# Optimizing a Trainium2 kernel written in Bass

```python
import numpy as np
import jax
import jax.numpy as jnp

def _softmax(x, axis=-1):
    return jax.nn.softmax(x, axis=axis)

def _gelu(x):
    return jax.nn.gelu(x, approximate=True)

def _silu(x):
    return jax.nn.silu(x)

def _sigmoid(x):
    return jax.nn.sigmoid(x)

def _layernorm(x, axis=-1, eps=1e-05):
    m = jnp.mean(x, axis=axis, keepdims=True)
    v = jnp.var(x, axis=axis, keepdims=True)
    return (x - m) / jnp.sqrt(v + eps)

def _scatter_add(tgt, idx, src, axis=0):
    return tgt.at[idx].add(src)

def _segment_sum(src, seg, n):
    return jax.ops.segment_sum(src, seg, n)
kernel_name = 'mk_cond_resid_d4_seqx_r8_66fecd'

def setup_inputs(seed: int=0):
    np.random.seed(seed)
    _w = jnp.asarray

    def _rec_inputs():
        import jax
        import jax.numpy as jnp
        _rk = jax.random.key(seed)
        x = 7.22e-05 + 1 * jax.random.normal(jax.random.fold_in(_rk, 1), (64, 32, 256), jnp.float32)
        _lenS = 32 - jax.random.randint(jax.random.fold_in(_rk, 7), (64,), 0, max(1, 32 // 4) + 1, jnp.int32)
        _lenS2 = 32 - jax.random.randint(jax.random.fold_in(_rk, 8), (64,), 0, max(1, 32 // 4) + 1, jnp.int32)
        cond_2048 = 0.0061147 + 1.02565 * jax.random.normal(jax.random.fold_in(_rk, 11), (64, 256), jnp.float32)
        return (x, cond_2048)
    x, cond_2048 = _rec_inputs()

    def _L0_cond_setup():
        import jax, jax.numpy as jnp
        import numpy as np
        DIM = 256
        H = 16
        DH = 128
        INNER = H * DH
        MLP = 4 * DIM
        B, T = (2, 256)
        EPS = 1e-06

        def _ln(x):
            mu = jnp.mean(x, axis=-1, keepdims=True)
            var = jnp.var(x, axis=-1, keepdims=True)
            return (x - mu) * jax.lax.rsqrt(var + EPS)
        key = jax.random.key(seed)
        ks = jax.random.split(key, 12)
        s = 0.02
        return {'x': jax.random.normal(ks[0], (B, T, DIM), jnp.float32), 'timestep_embed': jax.random.normal(ks[1], (B, DIM), jnp.float32), 'ada_w': jax.random.normal(ks[2], (DIM, 6 * DIM), jnp.float32) * s, 'ada_b': jnp.zeros((6 * DIM,), jnp.float32), 'qkv_w': jax.random.normal(ks[3], (DIM, 3 * INNER), jnp.float32) * s, 'qkv_b': jnp.zeros((3 * INNER,), jnp.float32), 'out_w': jax.random.normal(ks[4], (INNER, DIM), jnp.float32) * s, 'out_b': jnp.zeros((DIM,), jnp.float32), 'ffn_w1': jax.random.normal(ks[5], (DIM, MLP), jnp.float32) * s, 'ffn_b1': jnp.zeros((MLP,), jnp.float32), 'ffn_w2': jax.random.normal(ks[6], (MLP, DIM), jnp.float32) * s, 'ffn_b2': jnp.zeros((DIM,), jnp.float32)}
    _L0_cond_all = _L0_cond_setup()
    _L0_cond_in = {k: v for k, v in _L0_cond_all.items() if k in ('ada_w', 'ada_b', 'qkv_w', 'qkv_b', 'out_w', 'out_b', 'ffn_w1', 'ffn_b1', 'ffn_w2', 'ffn_b2')}
    del _L0_cond_all

    def _L1_cond_setup():
        import jax, jax.numpy as jnp
        import numpy as np
        B, T, D = (16, 128, 256)
        key = jax.random.key(seed)
        k0, k1, k2, k3 = jax.random.split(key, 4)
        scale = 1.0 / np.sqrt(D)
        return {'initial_state': jax.random.normal(k0, (B, D), jnp.float32), 'inputs': jax.random.normal(k1, (B, T, D), jnp.float32), 'W_ih': jax.random.normal(k2, (D, 3 * D), jnp.float32) * scale, 'W_hh': jax.random.normal(k3, (D, 3 * D), jnp.float32) * scale, 'b_ih': jnp.zeros((3 * D,), jnp.float32), 'b_hh': jnp.zeros((3 * D,), jnp.float32)}
    _L1_cond_all = _L1_cond_setup()
    _L1_cond_in = {k: v for k, v in _L1_cond_all.items() if k in ('W_ih', 'W_hh', 'b_ih', 'b_hh')}
    del _L1_cond_all

    def _L2_cond_setup():
        import jax, jax.numpy as jnp
        import numpy as np
        NUM_BLOCKS = 8
        NUM_LAYERS = 4
        EPS = 1e-06
        key = jax.random.key(seed)
        ks = jax.random.split(key, 6)
        B, S, H = (4, 512, 256)
        inputs = jax.random.normal(ks[0], (B, S, H), dtype=jnp.float32)
        query_vectors = jax.random.normal(ks[1], (NUM_LAYERS, H), dtype=jnp.float32) * 0.01
        lim = float(np.sqrt(6.0 / (H + H)))
        Wk = jax.random.uniform(ks[2], (H, H), minval=-lim, maxval=lim, dtype=jnp.float32)
        Wo = jax.random.uniform(ks[3], (H, H), minval=-lim, maxval=lim, dtype=jnp.float32)
        rms_weight = jnp.ones((H,), dtype=jnp.float32)
        ln_gamma = jnp.ones((H,), dtype=jnp.float32)
        ln_beta = jnp.zeros((H,), dtype=jnp.float32)
        return {'inputs': inputs, 'layer_idx': 1, 'rms_weight': rms_weight, 'query_vectors': query_vectors, 'Wk': Wk, 'Wo': Wo, 'ln_gamma': ln_gamma, 'ln_beta': ln_beta}
    _L2_cond_all = _L2_cond_setup()
    _L2_cond_in = {k: v for k, v in _L2_cond_all.items() if k in ('rms_weight', 'Wk', 'Wo', 'ln_gamma', 'ln_beta')}
    del _L2_cond_all

    def _L3_cond_setup():
        import jax, jax.numpy as jnp
        import numpy as np
        DT = 0.01
        EPSILON = 0.08
        ALPHA = 0.7
        BETA = 0.8
        CLAMP = 20.0
        B, T, N = (32, 128, 256)

        def _derivative(q, p, drive, coupling, bias):
            i_couple = jnp.tanh(q) @ coupling.T
            dq = q - q ** 3 / 3.0 - p + drive + i_couple + bias
            dp = EPSILON * (q + ALPHA - BETA * p)
            return (dq, dp)

        def _rk4_step(q, p, drive, coupling, bias):
            dq1, dp1 = _derivative(q, p, drive, coupling, bias)
            dq2, dp2 = _derivative(q + 0.5 * DT * dq1, p + 0.5 * DT * dp1, drive, coupling, bias)
            dq3, dp3 = _derivative(q + 0.5 * DT * dq2, p + 0.5 * DT * dp2, drive, coupling, bias)
            dq4, dp4 = _derivative(q + DT * dq3, p + DT * dp3, drive, coupling, bias)
            q_next = q + DT / 6.0 * (dq1 + 2 * dq2 + 2 * dq3 + dq4)
            p_next = p + DT / 6.0 * (dp1 + 2 * dp2 + 2 * dp3 + dp4)
            q_next = jnp.clip(q_next, -CLAMP, CLAMP)
            p_next = jnp.clip(p_next, -CLAMP, CLAMP)
            return (q_next, p_next)
        key = jax.random.key(seed)
        k1, k2, k3, k4 = jax.random.split(key, 4)
        return {'q0': jax.random.normal(k1, (B, N), dtype=jnp.float32), 'p0': jax.random.normal(k2, (B, N), dtype=jnp.float32), 'input_drive_seq': jax.random.normal(k3, (B, T, N), dtype=jnp.float32), 'coupling': jax.random.normal(k4, (N, N), dtype=jnp.float32) * 0.01, 'bias': jnp.zeros((N,), dtype=jnp.float32)}
    _L3_cond_all = _L3_cond_setup()
    _L3_cond_in = {k: v for k, v in _L3_cond_all.items() if k in ('coupling', 'bias')}
    del _L3_cond_all
    return {'x': x, 'cond_2048': cond_2048, 'L0_cond_ada_w': _L0_cond_in['ada_w'], 'L0_cond_ada_b': _L0_cond_in['ada_b'], 'L0_cond_qkv_w': _L0_cond_in['qkv_w'], 'L0_cond_qkv_b': _L0_cond_in['qkv_b'], 'L0_cond_out_w': _L0_cond_in['out_w'], 'L0_cond_out_b': _L0_cond_in['out_b'], 'L0_cond_ffn_w1': _L0_cond_in['ffn_w1'], 'L0_cond_ffn_b1': _L0_cond_in['ffn_b1'], 'L0_cond_ffn_w2': _L0_cond_in['ffn_w2'], 'L0_cond_ffn_b2': _L0_cond_in['ffn_b2'], 'L1_cond_W_ih': _L1_cond_in['W_ih'], 'L1_cond_W_hh': _L1_cond_in['W_hh'], 'L1_cond_b_ih': _L1_cond_in['b_ih'], 'L1_cond_b_hh': _L1_cond_in['b_hh'], 'L2_cond_rms_weight': _L2_cond_in['rms_weight'], 'L2_cond_Wk': _L2_cond_in['Wk'], 'L2_cond_Wo': _L2_cond_in['Wo'], 'L2_cond_ln_gamma': _L2_cond_in['ln_gamma'], 'L2_cond_ln_beta': _L2_cond_in['ln_beta'], 'L3_cond_coupling': _L3_cond_in['coupling'], 'L3_cond_bias': _L3_cond_in['bias']}

def reference(x, cond_2048, L0_cond_ada_w, L0_cond_ada_b, L0_cond_qkv_w, L0_cond_qkv_b, L0_cond_out_w, L0_cond_out_b, L0_cond_ffn_w1, L0_cond_ffn_b1, L0_cond_ffn_w2, L0_cond_ffn_b2, L1_cond_W_ih, L1_cond_W_hh, L1_cond_b_ih, L1_cond_b_hh, L2_cond_rms_weight, L2_cond_Wk, L2_cond_Wo, L2_cond_ln_gamma, L2_cond_ln_beta, L3_cond_coupling, L3_cond_bias):
    import jax
    import jax.numpy as jnp

    def _L0_cond_ref(x, timestep_embed, ada_w, ada_b, qkv_w, qkv_b, out_w, out_b, ffn_w1, ffn_b1, ffn_w2, ffn_b2):
        import jax, jax.numpy as jnp
        import numpy as np
        DIM = 256
        H = 16
        DH = 128
        INNER = H * DH
        MLP = 4 * DIM
        B, T = (2, 256)
        EPS = 1e-06

        def _ln(x):
            mu = jnp.mean(x, axis=-1, keepdims=True)
            var = jnp.var(x, axis=-1, keepdims=True)
            return (x - mu) * jax.lax.rsqrt(var + EPS)
        Bc, Tc, D = x.shape
        ada = (timestep_embed @ ada_w + ada_b)[:, None, :]
        shift1, scale1, gate1, shift2, scale2, gate2 = jnp.split(ada, 6, axis=-1)
        x1 = _ln(x) * (1.0 + scale1) + shift1
        qkv = (x1 @ qkv_w + qkv_b).reshape(Bc, Tc, 3, H, DH)
        q, k, v = (qkv[:, :, 0], qkv[:, :, 1], qkv[:, :, 2])
        scale = DH ** (-0.5)
        attn = jnp.einsum('bthd,bshd->bhts', q, k) * scale
        attn = jax.nn.softmax(attn, axis=-1)
        attn_out = jnp.einsum('bhts,bshd->bthd', attn, v).reshape(Bc, Tc, INNER)
        attn_out = attn_out @ out_w + out_b
        x = x + gate1 * attn_out
        x2 = _ln(x) * (1.0 + scale2) + shift2
        h = jax.nn.gelu(x2 @ ffn_w1 + ffn_b1, approximate=False)
        x = x + gate2 * (h @ ffn_w2 + ffn_b2)
        return x

    def _L1_cond_ref(initial_state, inputs, W_ih, W_hh, b_ih, b_hh):
        import jax, jax.numpy as jnp
        import numpy as np
        B, T, D = (16, 128, 256)
        "ScanOverTime(GRU cell): sequential per-timestep module call with\n            dict-state passing; merge_dict_trees stacks the per-step\n            'state_predicted' tensors along axis=1 -> [B, T, D]."

        def cell(h, x):
            gi = x @ W_ih + b_ih
            gh = h @ W_hh + b_hh
            i_r, i_z, i_n = jnp.split(gi, 3, axis=-1)
            h_r, h_z, h_n = jnp.split(gh, 3, axis=-1)
            r = jax.nn.sigmoid(i_r + h_r)
            z = jax.nn.sigmoid(i_z + h_z)
            n = jnp.tanh(i_n + r * h_n)
            h_new = (1.0 - z) * n + z * h
            return (h_new, h_new)
        xs = jnp.swapaxes(inputs, 0, 1)
        _, hs = jax.lax.scan(cell, initial_state, xs)
        return jnp.swapaxes(hs, 0, 1)

    def _L2_cond_ref(inputs, layer_idx, rms_weight, query_vectors, Wk, Wo, ln_gamma, ln_beta):
        import jax, jax.numpy as jnp
        import numpy as np
        NUM_BLOCKS = 8
        NUM_LAYERS = 4
        EPS = 1e-06
        B, S, H = inputs.shape
        block_size = max(1, S // NUM_BLOCKS)
        n_blocks = S // block_size
        block_repr = inputs.reshape(B, n_blocks, block_size, H).sum(axis=2)
        keys = jnp.einsum('bnh,kh->bnk', block_repr, Wk)
        rms = jnp.sqrt(jnp.mean(keys * keys, axis=-1, keepdims=True) + EPS)
        keys = keys / rms * rms_weight
        q = query_vectors[layer_idx]
        scores = jnp.einsum('bnh,h->bn', keys, q)
        attn = jax.nn.softmax(scores, axis=-1)
        attended = jnp.einsum('bn,bnh->bh', attn, block_repr)
        attended = jnp.broadcast_to(attended[:, None, :], (B, S, H))
        proj = jnp.einsum('bsh,kh->bsk', attended, Wo)
        x = inputs + proj
        mu = jnp.mean(x, axis=-1, keepdims=True)
        var = jnp.mean((x - mu) ** 2, axis=-1, keepdims=True)
        out = (x - mu) / jnp.sqrt(var + EPS) * ln_gamma + ln_beta
        return out

    def _L3_cond_ref(q0, p0, input_drive_seq, coupling, bias):
        import jax, jax.numpy as jnp
        import numpy as np
        DT = 0.01
        EPSILON = 0.08
        ALPHA = 0.7
        BETA = 0.8
        CLAMP = 20.0
        B, T, N = (32, 128, 256)

        def _derivative(q, p, drive, coupling, bias):
            i_couple = jnp.tanh(q) @ coupling.T
            dq = q - q ** 3 / 3.0 - p + drive + i_couple + bias
            dp = EPSILON * (q + ALPHA - BETA * p)
            return (dq, dp)

        def _rk4_step(q, p, drive, coupling, bias):
            dq1, dp1 = _derivative(q, p, drive, coupling, bias)
            dq2, dp2 = _derivative(q + 0.5 * DT * dq1, p + 0.5 * DT * dp1, drive, coupling, bias)
            dq3, dp3 = _derivative(q + 0.5 * DT * dq2, p + 0.5 * DT * dp2, drive, coupling, bias)
            dq4, dp4 = _derivative(q + DT * dq3, p + DT * dp3, drive, coupling, bias)
            q_next = q + DT / 6.0 * (dq1 + 2 * dq2 + 2 * dq3 + dq4)
            p_next = p + DT / 6.0 * (dp1 + 2 * dp2 + 2 * dp3 + dp4)
            q_next = jnp.clip(q_next, -CLAMP, CLAMP)
            p_next = jnp.clip(p_next, -CLAMP, CLAMP)
            return (q_next, p_next)
        drive_tbn = jnp.swapaxes(input_drive_seq, 0, 1)

        def scan_fn(carry, drive):
            q, p = carry
            q, p = _rk4_step(q, p, drive, coupling, bias)
            return ((q, p), q)
        (_, _), q_trace_tbn = jax.lax.scan(scan_fn, (q0, p0), drive_tbn)
        return jnp.swapaxes(q_trace_tbn, 0, 1)
    x = x + _L0_cond_ref(x, cond_2048, L0_cond_ada_w, L0_cond_ada_b, L0_cond_qkv_w, L0_cond_qkv_b, L0_cond_out_w, L0_cond_out_b, L0_cond_ffn_w1, L0_cond_ffn_b1, L0_cond_ffn_w2, L0_cond_ffn_b2)
    x = x + _L1_cond_ref(cond_2048, x, L1_cond_W_ih, L1_cond_W_hh, L1_cond_b_ih, L1_cond_b_hh)
    x = x + _L2_cond_ref(x, 1, L2_cond_rms_weight, cond_2048, L2_cond_Wk, L2_cond_Wo, L2_cond_ln_gamma, L2_cond_ln_beta)
    x = x + _L3_cond_ref(cond_2048, cond_2048, x, L3_cond_coupling, L3_cond_bias)
    return x

_drawn_inputs = setup_inputs


def setup_inputs(seed=0):
    import zlib

    import numpy as np

    out = dict(_drawn_inputs(seed))
    spreads = {'L0_cond_ada_b': (0.0, 0.416),
     'L0_cond_qkv_b': (0.0, 0.379),
     'L0_cond_out_b': (0.0, 0.329),
     'L0_cond_ffn_b1': (0.0, 0.8),
     'L0_cond_ffn_b2': (0.0, 0.305),
     'L1_cond_b_ih': (0.0, 0.1),
     'L1_cond_b_hh': (0.0, 0.1),
     'L2_cond_rms_weight': (1.0, 0.2),
     'L2_cond_ln_gamma': (1.0, 0.2),
     'L2_cond_ln_beta': (0.0, 0.1),
     'L3_cond_bias': (0.0, 0.8)}
    factors = {'L3_cond_coupling': 8.0}
    for name, (base, spread) in spreads.items():
        noise = np.random.default_rng([zlib.crc32(name.encode()), seed]).standard_normal(out[name].shape)
        drawn = base * np.exp(spread * noise) if base else spread * noise
        out[name] = jnp.asarray(drawn.astype(out[name].dtype))
    for name, factor in factors.items():
        out[name] = (out[name] * factor).astype(out[name].dtype)
    return out
```

```python
import numpy as np
import concourse.bass as bass
from concourse import mybir

F32 = mybir.dt.float32
F32R = mybir.dt.float32r
BF16 = mybir.dt.bfloat16
ACT = mybir.ActivationFunctionType
ALU = mybir.AluOpType
AX = mybir.AxisListType

P = 128
B, T, D = 64, 32, 256
KC = D // P
TOK = B * T
NG = 4
GT = TOK // NG
GB = B // NG
NT = GT // P
BT = P // T
HEADS, DH = 16, 128
NU = 4
HU = HEADS // NU
INNER = HEADS * DH
MLP = 4 * D
MC = MLP // P
NBLK, BLK = 8, T // 8
DT, EPSILON, ALPHA, BETA, CLAMP = 0.01, 0.08, 0.7, 0.8, 20.0
LN_EPS = 1e-6
A_P = EPSILON * DT / 2
WARM_GRU, WARM_RK = 28, 16

VEC = {}
_at = 0
for _name, _n in (("ada_b", 12), ("qkv_b", 48), ("out_b", 2), ("ffn_b1", 8), ("ffn_b2", 2), ("b_ih", 6),
                  ("b_hh", 6), ("rms_w", 2), ("ln_gamma", 2), ("ln_beta", 2), ("l3_bias", 2)):
    VEC[_name] = _at
    _at += _n
NVEC = _at
SHIFT1, SCALE1, GATE1, SHIFT2, SCALE2, GATE2 = range(6)

SOFT = ("max", "sub", "sum", "recip", "norm", "tr0", "tr1", "tr2", "tr3")
GATE = ("gate0", "add0", "gate1", "add1")
GRU_DVE = ("pre_r", "pre_z", "r_bias", "n_base", "z_h", "r_hn", "pre_n", "zc_n", "h")
GRU_ACT = ("r", "z", "zc", "n")
GRU_PE = ("r", "z", "hn")
RK_ACT = ("tanh", "square")
RK_DVE = ("Z1", "w1", "B1", "M1", "e2", "q2",
          "Z2", "w2", "B2", "M2", "e3", "q3",
          "Z3", "w3", "R", "B3", "M3", "e4", "q4",
          "Z4", "S3", "w4", "B4", "S4", "p_raw", "q_raw", "q", "p", "e1")
RK_POOL = ("Ea", "Eb", "rows", "R1", "R1t", "S1", "S1b", "S2")
RK_START = 3


def at(step, events, name):
    return step * len(events) + events.index(name) + 1


def build(nc, xT, cond, ada_w, qkv_w, out_w, ffn_w1, ffn_w2, w_ih, w_hh, wk, wo, coup, vecs, out):
    from contextlib import ExitStack

    ctx = ExitStack()
    base = (nc.sbuf_base + 127) // 128 * 128
    end = nc.sbuf_usable_end
    KB = 1024

    def place(name, shape, dtype, offset):
        size = (int(np.prod(shape[1:])) * (2 if dtype == BF16 else 4) + 31) // 32 * 32
        assert offset + size <= end, (name, offset + size, end)
        return nc.alloc_sbuf_tensor_at(name, shape, dtype, offset=offset), offset + size

    def row(at_, *tiles):
        made = []
        for name, shape, dtype in tiles:
            t, at_ = place(name, shape, dtype, at_)
            made.append(t)
        return (*made, at_)

    with ctx:
        x_all, ada, vec, cnd, ones, eps_t, gb, idle, perm = row(
            base, ("x_all", [P, KC, TOK], F32), ("ada", [P, 12, B], F32), ("vec", [P, NVEC], F32),
            ("cnd", [P, KC, B], F32), ("ones", [P, P], F32),
            ("eps_t", [P, 8], F32), ("gb", [P, 8], F32), ("idle", [P, P], BF16))
        W_hi, W_lo, a_w = row(perm, ("W_hi", [P, NU, KC, 3, HU * DH], F32R), ("W_lo", [P, NU, KC, 3, HU * DH], F32R))
        (wo_hi, wo_lo, stage, xc, sq, rs, x_hi, x_lo, qk, V, Pr, BD, o_hi, o_lo, mx, sm, a_end) = row(
            a_w, ("wo_hi", [P, HEADS, D], F32R), ("wo_lo", [P, HEADS, D], F32R), ("stage", [P, 3, HU * DH], F32),
            ("xc", [P, KC, GT], F32), ("sq", [P, KC, GT], F32), ("rs", [P, GT], F32),
            ("x_hi", [P, KC, GT], F32R), ("x_lo", [P, KC, GT], F32R),
            ("qk", [P, 2, 2, GT], F32), ("V", [P, NT, HU * DH], F32), ("Pr", [P, NT * HU, T], F32),
            ("BD", [P, NT * HU, P], F32), ("o_hi", [P, 2, GT], F32R), ("o_lo", [P, 2, GT], F32R),
            ("mx", [P, NT * HU], F32), ("sm", [P, NT * HU], F32))
        q_off = perm + 2 * 48 * KB + 32 * KB + 6 * KB + 4 * KB * 2 + 2 * KB + 8 * KB
        ada_sb, _ = place("ada_sb", [P, KC, 6 * D], F32, q_off)
        (f1_raw, f2_raw, f1_hi, f1_lo, f2_hi, f2_lo, m_hi, m_lo, g_hi, g_lo, f_w) = row(
            perm, ("f1_raw", [P, KC, MLP], F32), ("f2_raw", [P, MC, D], F32),
            ("f1_hi", [P, KC, MLP], F32R), ("f1_lo", [P, KC, MLP], F32R),
            ("f2_hi", [P, MC, D], F32R), ("f2_lo", [P, MC, D], F32R),
            ("m_hi", [P, KC, GT], F32R), ("m_lo", [P, KC, GT], F32R),
            ("g_hi", [P, MC, GT], F32R), ("g_lo", [P, MC, GT], F32R))
        assert f_w <= a_w
        (xtb, xorig, fc, fsq, frs, gel, ysc, ih_raw, hh, ih_hi, ih_lo, wk_sb, wo_sb, cp, f_end) = row(
            a_w, ("xtb", [P, KC, T, B], F32), ("xorig", [P, KC, TOK], F32), ("fc", [P, KC, GT], F32),
            ("fsq", [P, KC, GT], F32), ("frs", [P, GT], F32), ("gel", [P, 2, GT], F32), ("ysc", [P, GT], F32),
            ("ih_raw", [P, KC, 3 * D], F32), ("hh", [P, KC, 3 * D], F32),
            ("ih_hi", [P, KC, 3 * D], F32R), ("ih_lo", [P, KC, 3 * D], F32R),
            ("wk_sb", [P, KC, D], F32), ("wo_sb", [P, KC, D], F32), ("cp", [P, KC, D], F32))
        (gi, y_hi, y_lo, ht, ar, az, rg, zg, zcg, ng, rb, nb, zh, rn, pn, zn, bhn, g_end) = row(
            perm, ("gi", [P, 6, T, B], F32), ("y_hi", [P, KC, TOK], F32R), ("y_lo", [P, KC, TOK], F32R),
            ("ht", [P, KC, B], F32), *[(n, [P, KC, B], F32) for n in (
                "ar", "az", "rg", "zg", "zcg", "ng", "rb", "nb", "zh", "rn", "pn", "zn", "bhn")])
        (yt, h_all, g_all, d_all, blk, keys, keys2, wqr, s_rs, s_sc, s_at, s_mx, s_wb, att, l_end) = row(
            perm, ("yt", [P, KC, T, B], F32), ("h_all", [P, KC, T, B], F32), ("g_all", [P, KC, T + 1, B], F32),
            ("d_all", [P, KC, T + 1, B], F32),
            ("blk", [P, KC, NBLK, B], F32), ("keys", [P, KC, NBLK * B], F32), ("keys2", [P, KC, NBLK * B], F32),
            ("wqr", [P, KC, P], F32), ("s_rs", [P, NBLK * B], F32), ("s_sc", [P, NBLK, B], F32),
            ("s_at", [P, NBLK, B], F32), ("s_mx", [P, 2, B], F32), ("s_wb", [P, NBLK, B], F32),
            ("att", [P, KC, B], F32))
        assert g_end <= a_w and l_end <= a_w
        RKN = ("q", "th", "qsq", "w", "Bk", "Z", "e_a", "e_b", "e_c", "e_d", "M", "Ea", "Eb", "R1", "R",
               "R1t", "S1", "S1b", "S2", "S3", "S4", "pr", "p", "third", "g_row", "h_row", "d_row", "qraw", "q2", "q3", "q4")
        rk = {}
        off = a_w + 16 * KB
        for n in RKN:
            rk[n], off = place("rk_" + n, [P, KC, B], F32, off)
        assert off <= a_w + 32 * KB

        ps = ctx.enter_context(nc.psum_tensor("ps", [P, 8, 512], F32))
        PJ = (0, 1)
        SB = 2
        OB = (3, 4)
        YB = (5, 6)
        TB = 7

        def sem(name):
            return ctx.enter_context(nc.semaphore(name))

        ld_x, ld_x0, ld_v, ld_ada = sem("ld_x"), sem("ld_x0"), sem("ld_v"), sem("ld_ada")
        ld_w = [sem(f"ld_w{i}") for i in range(2)]
        ld_stage, ld_ffn, ld_late = sem("ld_stage"), sem("ld_ffn"), sem("ld_late")
        consts, ada_mm, ada_dn, w_hi0, w_rdy, pool_w, wo_rdy = (sem(n) for n in (
            "consts", "ada_mm", "ada_dn", "w_hi0", "w_rdy", "pool_w", "wo_rdy"))
        ln_pe, ln_dve, ln_act, ln_pool, x1_hi, x1_lo = (sem(n) for n in (
            "ln_pe", "ln_dve", "ln_act", "ln_pool", "x1_hi", "x1_lo"))
        proj_done, act_evac, dve_evac, scores_done, soft, exp_done = (sem(n) for n in (
            "proj_done", "act_evac", "dve_evac", "scores_done", "soft", "exp_done"))
        pv_done, ohi_done, olo_done, out_done, gate_done = (sem(n) for n in (
            "pv_done", "ohi_done", "olo_done", "out_done", "gate_done"))
        l2_pe, l2_dve, l2_act, l2_pool, m_hi_s, m_lo_s, fw_hi, fw_lo = (sem(n) for n in (
            "l2_pe", "l2_dve", "l2_act", "l2_pool", "m_hi_s", "m_lo_s", "fw_hi", "fw_lo"))
        up_done, gel_done, glo_done, down_done, fgate, ffn_out = (sem(n) for n in (
            "up_done", "gel_done", "glo_done", "down_done", "fgate", "ffn_out"))
        iw_hi, iw_lo, y_split, gi_mm, gi_act = (sem(n) for n in (
            "iw_hi", "iw_lo", "y_split", "gi_mm", "gi_act"))
        h0, gru_pe, gru_act, gru_dve, gru_out = (sem(n) for n in ("h0", "gru_pe", "gru_act", "gru_dve", "gru_out"))
        p_pe, p_dve, p_act, p_pool = (sem(n) for n in ("p_pe", "p_dve", "p_act", "p_pool"))
        rk_pe, rk_act, rk_dve, rk_pool, rk_out, rk0, stored = (sem(n) for n in (
            "rk_pe", "rk_act", "rk_dve", "rk_pool", "rk_out", "rk0", "stored"))

        def col(name, i):
            return vec[:, VEC[name] + i:VEC[name] + i + 1]

        def ada_rows(which, g, c=None):
            lo = 2 * which
            bs = bass.ds(g * GB, GB) if not isinstance(g, int) else slice(g * GB, g * GB + GB)
            if c is not None:
                return ada[:, lo + c, bs].unsqueeze(2).to_broadcast([P, GB, T])
            return ada[:, lo:lo + 2, bs].unsqueeze(3).to_broadcast([P, KC, GB, T])

        def group(tile, g, c=None):
            ts = bass.ds(g * GT, GT) if not isinstance(g, int) else slice(g * GT, g * GT + GT)
            return tile[:, :, ts] if c is None else tile[:, c, ts]

        def by_batch(ap):
            return ap.rearrange("p (b t) -> p b t", t=T)

        counts_from_one = {"pe": (pv_done, out_done, down_done, gi_mm),
                           "act": (gel_done, gi_act),
                           "dve": (olo_done, gate_done, glo_done, fgate, gru_dve, rk_dve),
                           "pool": (ffn_out, gru_out, rk_out)}

        def start_counts(engine, name):
            for s in counts_from_one[name]:
                engine.sem_inc(s, RK_START if s is rk_dve else 1)

        block = ctx.enter_context(nc.Block())

        @block.sync
        def _(sp):
            sp.dma_start(vec[:, :], vecs).then_inc(ld_v, 16)
            sp.dma_start(cnd[:, :, :], cond).then_inc(ld_v, 16)
            sp.dma_start(x_all[:, :, 0:GT], xT[:, :, 0:GT]).then_inc(ld_x0, 16)
            sp.dma_start(ada_sb[:, :, :], ada_w).then_inc(ld_ada, 16)
            sp.dma_start(BD[:, 0:12, :].rearrange("p a b -> p (a b)"), qkv_w[0, :, 0, :]).then_inc(ld_w[0], 16)
            sp.dma_start(stage[:, :, :].rearrange("p a b -> p (a b)"), qkv_w[0, :, 1, :]).then_inc(ld_w[1], 16)
            sp.dma_start(x_all[:, :, GT:TOK], xT[:, :, GT:TOK]).then_inc(ld_x, 16)
            n = 0
            for u in range(1, NU + 1):
                for kc in range(KC if u < NU else 0):
                    if n == 0:
                        sp.wait_ge(w_rdy, 2)
                    else:
                        sp.wait_ge(pool_w, 2 * n)
                    sp.dma_start(stage[:, :, :].rearrange("p a b -> p (a b)"),
                                 qkv_w[u, :, kc, :]).then_inc(ld_stage, 16)
                    n += 1
                sp.wait_ge(pool_w, 2 * n)
                sp.dma_start(stage[:, 0:2, :].rearrange("p a b -> p (a b)"),
                             out_w[:, HU * (u - 1) * D:HU * u * D]).then_inc(ld_stage, 16)
                n += 1
            sp.wait_ge(proj_done, 12 * NU * NG)
            sp.dma_start(f1_raw[:, :, :], ffn_w1).then_inc(ld_ffn, 16)
            sp.dma_start(f2_raw[:, :, :], ffn_w2).then_inc(ld_ffn, 16)
            sp.wait_ge(gate_done, 1 + len(GATE) * NG)
            sp.wait_ge(out_done, 1 + HEADS * NG)
            sp.dma_start(xorig[:, :, :], xT).then_inc(ld_late, 16)
            sp.dma_start(ih_raw[:, :, :], w_ih).then_inc(ld_late, 16)
            sp.dma_start(hh[:, :, :], w_hh).then_inc(ld_late, 16)
            sp.dma_start(wk_sb[:, :, :], wk).then_inc(ld_late, 16)
            sp.dma_start(wo_sb[:, :, :], wo).then_inc(ld_late, 16)
            sp.dma_start(cp[:, :, :], coup).then_inc(ld_late, 16)
            for i in range(4):
                sp.wait_ge(rk_out, 1 + 8 * (i + 1))
                sp.dma_start(out[:, :, 8 * i:8 * i + 8, :], xtb[:, :, 8 * i:8 * i + 8, :]).then_inc(stored, 16)
            sp.wait_ge(stored, 64)

        @block.tensor
        def _(pe):
            start_counts(pe, "pe")

            def three(out_, pairs, first=True, last=True):
                n = 3 * len(pairs)
                i = 0
                for lh, ll, rh, rl in pairs:
                    for lhsT, rhs in ((lh, rh), (ll, rh), (lh, rl)):
                        r = pe.matmul(out_, lhsT, rhs, start=first and i == 0, stop=last and i == n - 1)
                        i += 1
                return r

            def stat(src, s):
                for c in range(KC):
                    r = pe.matmul(ps[:, TB, :], ones[:, :], src[c], start=c == 0, stop=c == KC - 1)
                r.then_inc(s, 1)

            def ln_mean(g):
                if not isinstance(g, int) or g:
                    pe.wait_ge(ln_act, 2 * g)
                    pe.wait_ge(ld_x, 16)
                else:
                    pe.wait_ge(ld_x0, 16)
                stat([group(x_all, g, c) for c in range(KC)], ln_pe)

            def ln_var(g):
                pe.wait_ge(ln_act, 2 * g + 1)
                stat([sq[:, c, :] for c in range(KC)], ln_pe)

            def proj(n, ng, u, piece):
                kind, i = piece
                p = {"q": 2 * i, "k": 2 * i + 1, "v": 8 + i}[kind]
                if p == 0:
                    if u == 0:
                        pe.wait_ge(x1_lo, ng + 1)
                        pe.wait_ge(w_rdy, 2)
                    else:
                        pe.wait_ge(pool_w, 6 * u - 2)
                if p >= 2 or not (isinstance(n, int) and n == 0):
                    pe.wait_ge(act_evac if p % 2 == 0 else dve_evac, 6 * n + p // 2)
                o = ps[:, PJ[p % 2], :]
                if kind == "v":
                    ts = slice(i * P, i * P + P)
                    r = three(o, [(x_hi[:, c, ts], x_lo[:, c, ts], W_hi[:, u, c, 2, :], W_lo[:, u, c, 2, :])
                                  for c in range(KC)])
                else:
                    t, hs = "qk".index(kind), slice(i * DH, i * DH + DH)
                    r = three(o, [(W_hi[:, u, c, t, hs], W_lo[:, u, c, t, hs], x_hi[:, c, :], x_lo[:, c, :])
                                  for c in range(KC)])
                r.then_inc(proj_done, 1)

            def scores(n, h):
                pe.wait_ge(act_evac, 6 * n + h + 1)
                pe.wait_ge(dve_evac, 6 * n + h + 1)
                if h == 0 and not (isinstance(n, int) and n == 0):
                    pe.wait_ge(soft, len(SOFT) * (n - 1) + 2)
                for i in range(NT):
                    for j in range(BT):
                        t = slice(i * P + j * T, i * P + j * T + T)
                        r = pe.matmul(ps[j * T:j * T + T, SB, (i * HU + h) * T:(i * HU + h) * T + T],
                                      qk[:, 0, h % 2, t], qk[:, 1, h % 2, t], start=True, stop=True)
                r.then_inc(scores_done, 1)

            def pv(U, h):
                if h == 0:
                    pe.wait_ge(soft, len(SOFT) * (U + 1))
                    pe.wait_ge(act_evac, 6 * (U + 1))
                    pe.wait_ge(dve_evac, 6 * (U + 1))
                pe.wait_ge(olo_done, 1 + 4 * U + max(h - 1, 0))
                for i in range(NT):
                    r = pe.matmul(ps[:, OB[h % 2], i * P:i * P + P], V[:, i, h * DH:h * DH + DH],
                                  BD[:, i * HU + h, :], start=True, stop=True)
                r.then_inc(pv_done, 1)

            def head_sum(U, u, h, g):
                pe.wait_ge(olo_done, 1 + 4 * U + h + 1)
                if h == 0:
                    pe.wait_ge(pool_w, 6 * (u + 1) if u < 3 else 20)
                    if u == 0:
                        pe.wait_ge(gate_done, 1 + len(GATE) * g)
                k = HU * u + h
                for c in range(KC):
                    cs = slice(c * P, c * P + P)
                    r = three(ps[:, YB[c], :], [(wo_hi[:, k, cs], wo_lo[:, k, cs], o_hi[:, h % 2, :], o_lo[:, h % 2, :])],
                              first=k == 0, last=k == HEADS - 1)
                r.then_inc(out_done, 1)

            pe.wait_ge(consts, 1)
            ln_mean(0)
            pe.wait_ge(ld_v, 32)
            pe.wait_ge(ld_ada, 16)
            for j in range(12):
                for c in range(KC):
                    r = pe.matmul(ps[:, YB[j // 6], (j % 6) * B:(j % 6) * B + B], ada_sb[:, c, j * P:j * P + P],
                                  cnd[:, c, :], start=c == 0, stop=c == KC - 1)
            r.then_inc(ada_mm, 1)
            ln_var(0)

            FIRST = [("q", 0), ("k", 0), ("q", 1), ("k", 1), ("S", 0), ("q", 2), ("k", 2), ("S", 1), ("q", 3), ("k", 3),
                     ("S", 2), ("v", 0), ("S", 3), ("v", 1), ("v", 2), ("v", 3)]
            STEP = [("q", 0), ("k", 0), ("q", 1), ("k", 1), ("S", 0), ("q", 2), ("k", 2), ("S", 1), ("PV", 0), ("q", 3),
                    ("PV", 1), ("k", 3), ("Y", 0), ("S", 2), ("PV", 2), ("Y", 1), ("PV", 3), ("S", 3), ("v", 0),
                    ("Y", 2), ("v", 1), ("v", 2), ("v", 3), ("Y", 3)]

            def run(order, U, u, g, project):
                n = U + 1 if U is not None else 0
                ng = 0 if U is None else g if u < NU - 1 else g + 1
                un = (u + 1) % NU if U is not None else 0
                for kind, i in order:
                    if kind == "PV":
                        pv(U, i)
                    elif kind == "Y":
                        head_sum(U, u, i, g)
                    elif not project:
                        pass
                    elif kind == "S":
                        scores(n, i)
                    else:
                        proj(n, ng, un, (kind, i))

            run(FIRST, None, 0, 0, True)

            def attention(g, last):
                for u in range(NU):
                    U = NU * g + u
                    if not last and u == 0:
                        ln_mean(g + 1)
                    if not last and u == 1:
                        ln_var(g + 1)
                    run(STEP, U, u, g, not (last and u == NU - 1))

            with pe.Fori(0, NG - 1) as g:
                attention(g, False)
            attention(NG - 1, True)

            def l2_mean(g):
                if not isinstance(g, int) or g:
                    pe.wait_ge(l2_act, 2 * g)
                else:
                    pe.wait_ge(gate_done, 1 + len(GATE) * NG)
                    pe.wait_ge(ln_act, 2 * NG)
                stat([group(x_all, g, c) for c in range(KC)], l2_pe)

            def l2_var(g):
                pe.wait_ge(l2_act, 2 * g + 1)
                stat([fsq[:, c, :] for c in range(KC)], l2_pe)

            def ffn(g, last):
                pe.wait_ge(m_lo_s, g + 1)
                for m in range(MC):
                    if not last and m == 0:
                        l2_mean(g + 1)
                    if not last and m == 4:
                        l2_var(g + 1)
                    pe.wait_ge(gel_done, 1 + 2 * (MC * g + max(m - 1, 0)))
                    ms = slice(m * P, m * P + P)
                    three(ps[:, PJ[m % 2], :], [(f1_hi[:, c, ms], f1_lo[:, c, ms], m_hi[:, c, :], m_lo[:, c, :])
                                                for c in range(KC)]).then_inc(up_done, 1)
                for c in range(KC):
                    pe.wait_ge(fgate, 1 + KC * g)
                    cs = slice(c * P, c * P + P)
                    for m in range(MC):
                        if c == 0:
                            pe.wait_ge(glo_done, 1 + MC * g + m + 1)
                        r = three(ps[:, YB[c], :], [(f2_hi[:, m, cs], f2_lo[:, m, cs], g_hi[:, m, :], g_lo[:, m, :])],
                                  first=m == 0, last=m == MC - 1)
                    r.then_inc(down_done, 1)

            l2_mean(0)
            l2_var(0)
            pe.wait_ge(fw_lo, 2)
            with pe.Fori(0, NG - 1) as g:
                ffn(g, False)
            ffn(NG - 1, True)

            def keep_warm(n):
                for _ in range(n):
                    pe.matmul(ps[:, TB, 0:P], idle[:, :], idle[:, :], start=True, stop=True)

            def input_gates(j, m):
                if m == 0:
                    pe.wait_ge(y_split, 2 * j + 2)
                pe.wait_ge(gi_act, 1 + 6 * j + max(m - 1, 0))
                ms = slice(m * P, m * P + P)
                js = slice(0, GT) if isinstance(j, int) and j == 0 else bass.ds(GT * j, GT)
                three(ps[:, PJ[m % 2], :], [(ih_hi[:, c, ms], ih_lo[:, c, ms], y_hi[:, c, js], y_lo[:, c, js])
                                            for c in range(KC)]).then_inc(gi_mm, 1)

            def recur(t, j, s_, last):
                pe.wait_ge(gru_dve, 1 + len(GRU_DVE) * t)
                for part, bank in ((0, SB), (1, OB[0]), (2, OB[1])):
                    for c in range(KC):
                        ms = slice((KC * part + c) * P, (KC * part + c) * P + P)
                        for k in range(KC):
                            r = pe.matmul(ps[:, bank, c * B:c * B + B], hh[:, k, ms], ht[:, k, :],
                                          start=k == 0, stop=k == KC - 1)
                    r.then_inc(gru_pe, 1)
                if not last and s_ >= 2:
                    input_gates(j + 1, s_ - 2)
                else:
                    keep_warm(WARM_GRU)

            pe.wait_ge(iw_lo, 1)
            for m in range(6):
                input_gates(0, m)
            pe.wait_ge(h0, 1)
            with pe.Fori(0, NG - 1) as j:
                for s_ in range(8):
                    recur(8 * j + s_, j, s_, False)
            for s_ in range(8):
                recur(8 * (NG - 1) + s_, NG - 1, s_, True)

            pe.wait_ge(p_dve, 2)
            for c in range(KC):
                for k in range(KC):
                    r = pe.matmul(ps[:, PJ[c], :], wk_sb[:, k, c * P:c * P + P], blk[:, k, :, :].rearrange("p n b -> p (n b)"),
                                  start=k == 0, stop=k == KC - 1)
            r.then_inc(p_pe, 1)
            pe.wait_ge(p_dve, 5)
            for k in range(KC):
                r = pe.matmul(ps[:, SB, :], wqr[:, k, :], keys[:, k, :], start=k == 0, stop=k == KC - 1)
            r.then_inc(p_pe, 1)
            pe.wait_ge(p_act, 1)
            for k in range(KC):
                r = pe.matmul(ps[:, OB[0], :], ones[:, :], keys2[:, k, :], start=k == 0, stop=k == KC - 1)
            r.then_inc(p_pe, 1)
            pe.wait_ge(p_dve, 16)
            for c in range(KC):
                for k in range(KC):
                    r = pe.matmul(ps[:, OB[1], c * B:c * B + B], wo_sb[:, k, c * P:c * P + P], att[:, k, :],
                                  start=k == 0, stop=k == KC - 1)
            r.then_inc(p_pe, 1)
            for j in range(4):
                pe.wait_ge(p_dve, 18 + 3 * j)
                stat([yt[:, c, 8 * j:8 * j + 8, :].rearrange("p t b -> p (t b)") for c in range(KC)], p_pe)
                pe.wait_ge(p_act, 4 + 2 * j)
                stat([fsq[:, c, :] for c in range(KC)], p_pe)

            pe.wait_ge(rk0, 2)
            with pe.Fori(0, T) as t:
                for k in range(4):
                    pe.wait_ge(rk_act, 8 * t + 2 * k + 1)
                    for c in range(KC):
                        for kk in range(KC):
                            r = pe.matmul(ps[:, SB if k % 2 == 0 else OB[0], c * B:c * B + B], cp[:, kk, c * P:c * P + P],
                                          rk["th"][:, kk, :], start=kk == 0, stop=kk == KC - 1)
                    r.then_inc(rk_pe, 1)
                    keep_warm(WARM_RK)

        @block.scalar
        def _(act):
            start_counts(act, "act")

            def ln_square(g):
                act.wait_ge(ln_dve, 2 * g + 1)
                if not isinstance(g, int) or g:
                    act.wait_ge(ln_pe, 2 * g)
                act.activation(sq[:, :, :], xc[:, :, :], ACT.Square).then_inc(ln_act, 1)

            def ln_sqrt(g):
                act.wait_ge(ln_pe, 2 * g + 2)
                if not isinstance(g, int) or g:
                    act.wait_ge(ln_pool, 3 * g)
                act.activation(rs[:, :], ps[:, TB, :], ACT.Sqrt, bias=eps_t[:, 0:1]).then_inc(ln_act, 1)

            def high(g):
                act.wait_ge(ln_pool, 3 * g + 3)
                if not isinstance(g, int) or g:
                    act.wait_ge(proj_done, 48 * g)
                act.activation(x_hi[:, :, :], xc[:, :, :], ACT.Copy).then_inc(x1_hi, 1)

            def query(n, u, h):
                act.wait_ge(proj_done, 12 * n + 2 * h + 1)
                if h >= 2 or not (isinstance(n, int) and n == 0):
                    act.wait_ge(scores_done, 4 * n + h - 1)
                else:
                    act.wait_ge(ada_mm, 1)
                act.activation(qk[:, 0, h % 2, :], ps[:, PJ[0], :], ACT.Identity,
                               bias=col("qkv_b", HU * u + h)).then_inc(act_evac, 1)

            def value(n, i):
                act.wait_ge(proj_done, 12 * n + 8 + i + 1)
                if not (isinstance(n, int) and n == 0):
                    act.wait_ge(pv_done, 1 + 4 * n)
                act.activation(V[:, i, :], ps[:, PJ[0], :], ACT.Copy).then_inc(act_evac, 1)

            def exp(U):
                act.wait_ge(soft, len(SOFT) * U + 2)
                act.activation(Pr[:, :, :], Pr[:, :, :], ACT.Exp, scale=DH ** -0.5).then_inc(exp_done, 1)

            def out_high(U, u, h):
                act.wait_ge(pv_done, 1 + 4 * U + h + 1)
                act.wait_ge(out_done, 1 + 4 * U + max(h - 1, 0))
                act.activation(o_hi[:, h % 2, :], ps[:, OB[h % 2], :], ACT.Identity,
                               bias=col("qkv_b", 2 * HEADS + HU * u + h)).then_inc(ohi_done, 1)

            act.wait_ge(consts, 1)
            ln_square(0)
            ln_sqrt(0)
            for kc, src in enumerate((BD[:, 0:12, :].rearrange("p a b -> p (a b)"),
                                      stage[:, :, :].rearrange("p a b -> p (a b)"))):
                act.wait_ge(ld_w[kc], 16)
                act.activation(W_hi[:, 0, kc, :, :].rearrange("p a b -> p (a b)"), src, ACT.Copy).then_inc(w_hi0, 1)
            high(0)
            for h in range(HU):
                query(0, 0, h)
            value(0, 0)
            value(0, 2)

            def attention(g, last):
                for u in range(NU):
                    U = NU * g + u
                    n, un = U + 1, (u + 1) % NU
                    project = not (last and u == NU - 1)
                    if u == NU - 1 and not last:
                        high(g + 1)
                    if project:
                        query(n, un, 0)
                    exp(U)
                    if project:
                        query(n, un, 1)
                    if u == 0 and not last:
                        ln_square(g + 1)
                    if u == 1 and not last:
                        ln_sqrt(g + 1)
                    if project:
                        query(n, un, 2)
                    out_high(U, u, 0)
                    if project:
                        query(n, un, 3)
                    for h in range(1, HU):
                        out_high(U, u, h)
                    if project:
                        value(n, 0)
                        value(n, 2)

            with act.Fori(0, NG - 1) as g:
                attention(g, False)
            attention(NG - 1, True)

            def l2_square(g):
                act.wait_ge(l2_dve, 2 * g + 1)
                if not isinstance(g, int) or g:
                    act.wait_ge(l2_pe, 2 * g)
                act.activation(fsq[:, :, :], fc[:, :, :], ACT.Square).then_inc(l2_act, 1)

            def l2_sqrt(g):
                act.wait_ge(l2_pe, 2 * g + 2)
                if not isinstance(g, int) or g:
                    act.wait_ge(l2_pool, 3 * g)
                act.activation(frs[:, :], ps[:, TB, :], ACT.Sqrt, bias=eps_t[:, 0:1]).then_inc(l2_act, 1)

            def m_high(g):
                act.wait_ge(l2_pool, 3 * g + 3)
                if not isinstance(g, int) or g:
                    act.wait_ge(up_done, MC * g)
                act.activation(m_hi[:, :, :], fc[:, :, :], ACT.Copy).then_inc(m_hi_s, 1)

            def ffn(g, last):
                for m in range(MC):
                    act.wait_ge(up_done, MC * g + m + 1)
                    act.wait_ge(glo_done, 1 + MC * g + max(m - 1, 0))
                    act.activation(gel[:, m % 2, :], ps[:, PJ[m % 2], :], ACT.Gelu,
                                   bias=col("ffn_b1", m)).then_inc(gel_done, 1)
                    act.wait_ge(down_done, 1 + KC * g)
                    act.activation(g_hi[:, m, :], ps[:, PJ[m % 2], :], ACT.Gelu,
                                   bias=col("ffn_b1", m)).then_inc(gel_done, 1)
                    if m == 1 and not last:
                        l2_square(g + 1)
                    if m == 5 and not last:
                        l2_sqrt(g + 1)
                if not last:
                    m_high(g + 1)

            act.wait_ge(ld_ffn, 32)
            act.activation(f1_hi[:, :, :], f1_raw[:, :, :], ACT.Copy).then_inc(fw_hi, 1)
            act.activation(f2_hi[:, :, :], f2_raw[:, :, :], ACT.Copy).then_inc(fw_hi, 1)
            l2_square(0)
            l2_sqrt(0)
            m_high(0)
            with act.Fori(0, NG - 1) as g:
                ffn(g, False)
            ffn(NG - 1, True)

            act.wait_ge(ld_late, 96)
            act.activation(ih_hi[:, :, :], ih_raw[:, :, :], ACT.Copy).then_inc(iw_hi, 1)
            act.wait_ge(h0, 1)

            def gates_out(j, m):
                act.wait_ge(gi_mm, 1 + 6 * j + m + 1)
                ts = slice(0, 8) if isinstance(j, int) and j == 0 else bass.ds(8 * j, 8)
                act.activation(gi[:, m, ts, :].rearrange("p t b -> p (t b)"), ps[:, PJ[m % 2], :],
                               ACT.Identity, bias=gb[:, m:m + 1]).then_inc(gi_act, 1)

            for m in range(6):
                gates_out(0, m)

            def recur(t, j, s_, last):
                def wait_dve(name):
                    act.wait_ge(gru_dve, 1 + at(t, GRU_DVE, name))
                wait_dve("pre_r")
                act.activation(rg[:, :, :], ar[:, :, :], ACT.Sigmoid).then_inc(gru_act, 1)
                wait_dve("pre_z")
                act.activation(zg[:, :, :], az[:, :, :], ACT.Sigmoid).then_inc(gru_act, 1)
                act.activation(zcg[:, :, :], az[:, :, :], ACT.Sigmoid, scale=-1.0).then_inc(gru_act, 1)
                wait_dve("pre_n")
                act.activation(ng[:, :, :], pn[:, :, :], ACT.Tanh).then_inc(gru_act, 1)
                if not last and s_ >= 2:
                    gates_out(j + 1, s_ - 2)

            act.activation(gb[:, 6:7], gb[:, 0:1], ACT.Sigmoid)
            with act.Fori(0, NG - 1) as j:
                for s_ in range(8):
                    recur(8 * j + s_, j, s_, False)
            for s_ in range(8):
                recur(8 * (NG - 1) + s_, NG - 1, s_, True)

            act.wait_ge(p_dve, 5)
            act.activation(keys2[:, :, :], keys[:, :, :], ACT.Square).then_inc(p_act, 1)
            act.wait_ge(p_pe, 3)
            act.activation(s_rs[:, :], ps[:, OB[0], :], ACT.Sqrt, bias=eps_t[:, 0:1]).then_inc(p_act, 1)
            act.wait_ge(p_dve, 9)
            act.activation(s_at[:, :, :], s_at[:, :, :], ACT.Exp).then_inc(p_act, 1)
            for j in range(4):
                act.wait_ge(p_dve, 19 + 3 * j)
                if j:
                    act.wait_ge(p_pe, 4 + 2 * j)
                act.activation(fsq[:, :, :], fc[:, :, :], ACT.Square).then_inc(p_act, 1)
                act.wait_ge(p_pe, 6 + 2 * j)
                act.activation(frs[:, :], ps[:, TB, :], ACT.Sqrt, bias=eps_t[:, 0:1]).then_inc(p_act, 1)

            act.activation(gb[:, 7:8], gb[:, 0:1], ACT.Tanh)
            act.wait_ge(rk0, 2)
            with act.Fori(0, T) as t:
                for k in range(4):
                    qk_ = rk[("q", "q2", "q3", "q4")[k]]
                    if k:
                        act.wait_ge(rk_dve, RK_START + at(t, RK_DVE, ("q2", "q3", "q4")[k - 1]))
                    else:
                        act.wait_ge(rk_dve, RK_START + len(RK_DVE) * t - 2)
                    act.activation(rk["th"][:, :, :], qk_[:, :, :], ACT.Tanh).then_inc(rk_act, 1)
                    act.activation(rk["qsq"][:, :, :], qk_[:, :, :], ACT.Square).then_inc(rk_act, 1)

        @block.vector
        def _(dve):
            start_counts(dve, "dve")
            dve.memset(idle[:, :], 0.0)
            dve.memset(ones[:, :], 1.0 / D)
            dve.memset(eps_t[:, :], LN_EPS).then_inc(consts, 1)

            def ln_center(g):
                dve.wait_ge(ln_pe, 2 * g + 1)
                if not isinstance(g, int) or g:
                    dve.wait_ge(x1_lo, g)
                dve.tensor_tensor(xc[:, :, :], group(x_all, g),
                                  ps[:, TB, :].unsqueeze(1).to_broadcast([P, KC, GT]), ALU.subtract).then_inc(ln_dve, 1)

            def ln_recip(g):
                dve.wait_ge(ln_act, 2 * g + 2)
                dve.reciprocal(rs[:, :], rs[:, :]).then_inc(ln_dve, 1)

            def low(g):
                dve.wait_ge(x1_hi, g + 1)
                dve.tensor_tensor(x_lo[:, :, :], xc[:, :, :], x_hi[:, :, :].bitcast(F32), ALU.subtract).then_inc(x1_lo, 1)

            def key(n, u, h):
                dve.wait_ge(proj_done, 12 * n + 2 * h + 2)
                if h >= 2 or not (isinstance(n, int) and n == 0):
                    dve.wait_ge(scores_done, 4 * n + h - 1)
                dve.tensor_scalar(qk[:, 1, h % 2, :], ps[:, PJ[1], :], col("qkv_b", HEADS + HU * u + h), None,
                                  ALU.add).then_inc(dve_evac, 1)

            def value(n, i):
                dve.wait_ge(proj_done, 12 * n + 8 + i + 1)
                if not (isinstance(n, int) and n == 0):
                    dve.wait_ge(pv_done, 1 + 4 * n)
                dve.tensor_copy(V[:, i, :], ps[:, PJ[1], :]).then_inc(dve_evac, 1)

            def out_low(U, u, h):
                dve.wait_ge(ohi_done, 4 * U + h + 1)
                dve.scalar_tensor_tensor(o_lo[:, h % 2, :], ps[:, OB[h % 2], :], col("qkv_b", 2 * HEADS + HU * u + h),
                                         o_hi[:, h % 2, :].bitcast(F32), ALU.add, ALU.subtract).then_inc(olo_done, 1)

            def soft_wait(U, name):
                dve.wait_ge(soft, at(U, SOFT, name))

            S = ps[:, SB, :].rearrange("p (a s) -> p a s", s=T)
            whole = [P, NT * HU, T]

            def soft_a(U):
                dve.wait_ge(scores_done, 4 * U + 4)
                dve.reduce_max(mx[:, :], S, axis=AX.X).then_inc(soft, 1)
                soft_wait(U, "max")
                dve.tensor_tensor(Pr[:, :, :], S, mx[:, :].unsqueeze(2).to_broadcast(whole), ALU.subtract).then_inc(soft, 1)

            def soft_b(U):
                dve.wait_ge(exp_done, U + 1)
                dve.reduce_sum(sm[:, :], Pr[:, :, :], axis=AX.X).then_inc(soft, 1)
                soft_wait(U, "sum")
                dve.reciprocal(sm[:, :], sm[:, :]).then_inc(soft, 1)
                soft_wait(U, "recip")
                dve.tensor_tensor(Pr[:, :, :], Pr[:, :, :], sm[:, :].unsqueeze(2).to_broadcast(whole), ALU.mult).then_inc(soft, 1)

            def soft_c(U):
                soft_wait(U, "norm")
                dve.wait_ge(pv_done, 1 + 4 * U)
                for j in range(BT):
                    js = slice(j * T, j * T + T)
                    dve.transpose(BD[js, :, js], Pr[js, :, :]).then_inc(soft, 1)

            def gate(g):
                scratch = Pr[:, :, :].rearrange("p a s -> p (a s)")
                dve.wait_ge(out_done, 1 + 16 * g + 16)
                for c in range(KC):
                    if c:
                        dve.wait_ge(gate_done, 1 + at(g, GATE, "add0"))
                    dve.scalar_tensor_tensor(by_batch(scratch), by_batch(ps[:, YB[c], :]), col("out_b", c),
                                             ada_rows(GATE1, g, c), ALU.add, ALU.mult).then_inc(gate_done, 1)
                    dve.wait_ge(gate_done, 1 + at(g, GATE, f"gate{c}"))
                    dve.tensor_tensor(group(x_all, g, c), group(x_all, g, c), scratch, ALU.add).then_inc(gate_done, 1)

            ln_center(0)
            dve.wait_ge(ld_v, 32)
            dve.wait_ge(ada_mm, 1)
            for j in range(12):
                one = 1.0 if j // 2 in (SCALE1, SCALE2) else 0.0
                r = dve.tensor_scalar(ada[:, j, :], ps[:, YB[j // 6], (j % 6) * B:(j % 6) * B + B], col("ada_b", j), one,
                                      ALU.add, ALU.add)
            r.then_inc(ada_dn, 1)
            ln_recip(0)
            for kc, src in enumerate((BD[:, 0:12, :].rearrange("p a b -> p (a b)"),
                                      stage[:, :, :].rearrange("p a b -> p (a b)"))):
                dve.wait_ge(w_hi0, kc + 1)
                dve.tensor_tensor(W_lo[:, 0, kc, :, :].rearrange("p a b -> p (a b)"), src,
                                  W_hi[:, 0, kc, :, :].rearrange("p a b -> p (a b)").bitcast(F32),
                                  ALU.subtract).then_inc(w_rdy, 1)
            dve.wait_ge(w_rdy, 1)
            dve.memset(BD[:, :, :], 0.0).then_inc(ada_dn, 1)
            low(0)
            for h in range(HU):
                key(0, 0, h)
            value(0, 1)
            value(0, 3)
            dve.wait_ge(ada_dn, 2)

            def attention(g, last):
                for u in range(NU):
                    U = NU * g + u
                    n, un = U + 1, (u + 1) % NU
                    project = not (last and u == NU - 1)
                    if u == NU - 1 and not last:
                        low(g + 1)
                    soft_a(U)
                    if project:
                        key(n, un, 0)
                    soft_b(U)
                    if project:
                        key(n, un, 1)
                    if u == 0 and not last:
                        ln_center(g + 1)
                    if u == 1 and not last:
                        ln_recip(g + 1)
                    soft_c(U)
                    if project:
                        key(n, un, 2)
                    out_low(U, u, 0)
                    out_low(U, u, 1)
                    if project:
                        key(n, un, 3)
                    out_low(U, u, 2)
                    out_low(U, u, 3)
                    if project:
                        value(n, 1)
                        value(n, 3)
                    if u == NU - 1:
                        gate(g)

            with dve.Fori(0, NG - 1) as g:
                attention(g, False)
            attention(NG - 1, True)

            def l2_center(g):
                dve.wait_ge(l2_pe, 2 * g + 1)
                if not isinstance(g, int) or g:
                    dve.wait_ge(m_lo_s, g)
                dve.tensor_tensor(fc[:, :, :], group(x_all, g),
                                  ps[:, TB, :].unsqueeze(1).to_broadcast([P, KC, GT]), ALU.subtract).then_inc(l2_dve, 1)

            def l2_recip(g):
                dve.wait_ge(l2_act, 2 * g + 2)
                dve.reciprocal(frs[:, :], frs[:, :]).then_inc(l2_dve, 1)

            def m_low(g):
                dve.wait_ge(m_hi_s, g + 1)
                dve.tensor_tensor(m_lo[:, :, :], fc[:, :, :], m_hi[:, :, :].bitcast(F32), ALU.subtract).then_inc(m_lo_s, 1)

            def ffn(g, last):
                for m in range(MC):
                    dve.wait_ge(gel_done, 1 + 2 * (MC * g + m) + 2)
                    dve.tensor_tensor(g_lo[:, m, :], gel[:, m % 2, :], g_hi[:, m, :].bitcast(F32),
                                      ALU.subtract).then_inc(glo_done, 1)
                    if m == 1 and not last:
                        l2_center(g + 1)
                    if m == 5 and not last:
                        l2_recip(g + 1)
                if not last:
                    m_low(g + 1)
                for c in range(KC):
                    dve.wait_ge(down_done, 1 + KC * g + c + 1)
                    dve.wait_ge(ffn_out, 1 + 4 * g + 2 * c)
                    dve.scalar_tensor_tensor(by_batch(ysc[:, :]), by_batch(ps[:, YB[c], :]), col("ffn_b2", c),
                                             ada_rows(GATE2, g, c), ALU.add, ALU.mult).then_inc(fgate, 1)

            l2_center(0)
            l2_recip(0)
            dve.wait_ge(fw_hi, 1)
            dve.tensor_tensor(f1_lo[:, :, :], f1_raw[:, :, :], f1_hi[:, :, :].bitcast(F32), ALU.subtract).then_inc(fw_lo, 1)
            dve.wait_ge(fw_hi, 2)
            dve.tensor_tensor(f2_lo[:, :, :], f2_raw[:, :, :], f2_hi[:, :, :].bitcast(F32), ALU.subtract).then_inc(fw_lo, 1)
            m_low(0)
            with dve.Fori(0, NG - 1) as g:
                ffn(g, False)
            ffn(NG - 1, True)

            dve.wait_ge(iw_hi, 1)
            dve.tensor_tensor(ih_lo[:, :, :], ih_raw[:, :, :], ih_hi[:, :, :].bitcast(F32), ALU.subtract).then_inc(iw_lo, 1)
            dve.wait_ge(down_done, 1 + KC * NG)
            dve.wait_ge(glo_done, 1 + MC * NG)
            dve.tensor_copy(gb[:, 4:6], vec[:, VEC["b_ih"] + 4:VEC["b_ih"] + 6])
            dve.tensor_tensor(gb[:, 0:4], vec[:, VEC["b_ih"]:VEC["b_ih"] + 4], vec[:, VEC["b_hh"]:VEC["b_hh"] + 4], ALU.add)
            dve.tensor_copy(bhn[:, :, :], vec[:, VEC["b_hh"] + 4:VEC["b_hh"] + 6].unsqueeze(2).to_broadcast([P, KC, B]))
            dve.tensor_copy(ht[:, :, :], cnd[:, :, :]).then_inc(h0, 1)
            dve.wait_ge(h0, 1)
            def recur(t):
                def half(bank):
                    return ps[:, bank, 0:KC * B].rearrange("p (c b) -> p c b", b=B)

                def gates(part):
                    return gi[:, KC * part:KC * part + KC, bass.ds(t, 1), :].rearrange("p c t b -> p c (t b)")

                def mine(name):
                    dve.wait_ge(gru_dve, 1 + at(t, GRU_DVE, name))

                dve.wait_ge(gru_pe, at(t, GRU_PE, "r"))
                dve.tensor_tensor(ar[:, :, :], half(SB), gates(0), ALU.add).then_inc(gru_dve, 1)
                dve.wait_ge(gru_pe, at(t, GRU_PE, "z"))
                dve.tensor_tensor(az[:, :, :], half(OB[0]), gates(1), ALU.add).then_inc(gru_dve, 1)
                dve.wait_ge(gru_act, at(t, GRU_ACT, "r"))
                dve.tensor_tensor(rb[:, :, :], rg[:, :, :], bhn[:, :, :], ALU.mult).then_inc(gru_dve, 1)
                mine("r_bias")
                dve.tensor_tensor(nb[:, :, :], rb[:, :, :], gates(2), ALU.add).then_inc(gru_dve, 1)
                dve.wait_ge(gru_act, at(t, GRU_ACT, "z"))
                dve.tensor_tensor(zh[:, :, :], zg[:, :, :], ht[:, :, :], ALU.mult).then_inc(gru_dve, 1)
                dve.wait_ge(gru_pe, at(t, GRU_PE, "hn"))
                dve.tensor_tensor(rn[:, :, :], half(OB[1]), rg[:, :, :], ALU.mult).then_inc(gru_dve, 1)
                mine("r_hn")
                dve.tensor_tensor(pn[:, :, :], rn[:, :, :], nb[:, :, :], ALU.add).then_inc(gru_dve, 1)
                dve.wait_ge(gru_act, at(t, GRU_ACT, "n"))
                dve.tensor_tensor(zn[:, :, :], ng[:, :, :], zcg[:, :, :], ALU.mult).then_inc(gru_dve, 1)
                dve.wait_ge(gru_out, 1 + t)
                mine("zc_n")
                dve.tensor_tensor(ht[:, :, :], zn[:, :, :], zh[:, :, :], ALU.add).then_inc(gru_dve, 1)

            with dve.Fori(0, T // 8) as j:
                dve.wait_ge(gi_act, 1 + 6 * (j + 1))
                for s_ in range(8):
                    recur(8 * j + s_)

            dve.wait_ge(gru_out, 1 + T)
            dve.wait_ge(gru_dve, 1 + len(GRU_DVE) * T)
            seq = [0]

            def step(r):
                seq[0] += 1
                r.then_inc(p_dve, 1)

            def done():
                dve.wait_ge(p_dve, seq[0])

            for c in range(KC):
                step(dve.reduce_sum(blk[:, c, :, :], xtb[:, c, :, :].rearrange("p (n s) b -> p n b s", s=BLK), axis=AX.X))
            step(dve.tensor_tensor(s_mx[:, 0, 0:KC], vec[:, VEC["rms_w"]:VEC["rms_w"] + KC],
                                   cnd[:, :, 1], ALU.mult))
            done()
            step(dve.tensor_copy(wqr[:, :, :], s_mx[:, 0, 0:KC].unsqueeze(2).to_broadcast([P, KC, P])))
            dve.wait_ge(p_pe, 1)
            step(dve.tensor_copy(keys[:, :, :], ps[:, 0:2, :]))
            dve.wait_ge(p_act, 2)
            step(dve.reciprocal(s_rs[:, :], s_rs[:, :]))
            done()
            step(dve.tensor_tensor(s_sc[:, :, :].rearrange("p n b -> p (n b)"), ps[:, SB, :], s_rs[:, :], ALU.mult))
            done()
            step(dve.reduce_max(s_mx[:, 1, :], s_sc[:, :, :].rearrange("p n b -> p b n"), axis=AX.X))
            done()
            spread = [P, NBLK, B]
            step(dve.tensor_tensor(s_at[:, :, :], s_sc[:, :, :], s_mx[:, 1, :].unsqueeze(1).to_broadcast(spread),
                                   ALU.subtract))
            dve.wait_ge(p_act, 3)
            step(dve.reduce_sum(s_mx[:, 0, :], s_at[:, :, :].rearrange("p n b -> p b n"), axis=AX.X))
            done()
            step(dve.reciprocal(s_mx[:, 0, :], s_mx[:, 0, :]))
            done()
            step(dve.tensor_tensor(s_at[:, :, :], s_at[:, :, :], s_mx[:, 0, :].unsqueeze(1).to_broadcast(spread),
                                   ALU.mult))
            done()
            for c in range(KC):
                step(dve.tensor_tensor(s_wb[:, :, :], blk[:, c, :, :], s_at[:, :, :], ALU.mult))
                done()
                step(dve.reduce_sum(att[:, c, :], s_wb[:, :, :].rearrange("p n b -> p b n"), axis=AX.X))
                done()
            dve.wait_ge(p_pe, 4)
            for c in range(KC):
                step(dve.tensor_tensor(yt[:, c, :, :], xtb[:, c, :, :],
                                       ps[:, OB[1], c * B:c * B + B].unsqueeze(1).to_broadcast([P, T, B]), ALU.add))
            done()
            for j in range(4):
                js = slice(8 * j, 8 * j + 8)
                yj = yt[:, :, js, :].rearrange("p c t b -> p c (t b)")
                dve.wait_ge(p_pe, 5 + 2 * j)
                if j:
                    done()
                step(dve.tensor_tensor(fc[:, :, :], yj, ps[:, TB, :].unsqueeze(1).to_broadcast([P, KC, GT]), ALU.subtract))
                dve.wait_ge(p_act, 5 + 2 * j)
                step(dve.reciprocal(frs[:, :], frs[:, :]))
                done()
                step(dve.tensor_tensor(yj, fc[:, :, :], frs[:, :].unsqueeze(1).to_broadcast([P, KC, GT]), ALU.mult))

            dve.tensor_copy(rk["q"][:, :, :], cnd[:, :, :])
            dve.wait_ge(p_pool, 20)
            dve.tensor_tensor(rk["e_a"][:, :, :], d_all[:, :, 0, :], cnd[:, :, :], ALU.subtract).then_inc(rk0, 2)
            dve.wait_ge(rk0, 2)
            r_ = {n: rk[n][:, :, :] for n in rk}
            STT = dve.scalar_tensor_tensor
            with dve.Fori(0, T) as t:
                def mine(name):
                    dve.wait_ge(rk_dve, RK_START + at(t, RK_DVE, name))

                def pool(name):
                    dve.wait_ge(rk_pool, 1 + at(t, RK_POOL, name))

                def sq_done(k):
                    dve.wait_ge(rk_act, 8 * t + 2 * k + 2)

                def a_of(k):
                    return ps[:, SB if k % 2 == 0 else OB[0], 0:KC * B].rearrange("p (c b) -> p c b", b=B)

                def inc(r):
                    r.then_inc(rk_dve, 1)

                M, Ad = ALU.mult, ALU.add
                names = ("q", "q2", "q3", "q4")
                es = ("e_a", "e_b", "e_c", "e_d")
                coef = (DT / 2, DT / 2, DT)
                for k in range(3):
                    ck, pk = coef[k], coef[k] * EPSILON
                    if k:
                        mine(f"e{k + 1}")
                    else:
                        dve.wait_ge(rk_dve, RK_START + len(RK_DVE) * t)
                    inc(STT(r_["Z"], r_[es[k]], ck, r_["q"], M, Ad))
                    sq_done(k)
                    inc(STT(r_["w"], r_["qsq"], -3.0, r_[names[k]], Ad, M))
                    if k == 2:
                        pool("R1t")
                        inc(STT(r_["R"], r_["q3"], 2 / 3, r_["R1t"], M, Ad))
                    mine(f"w{k + 1}")
                    inc(STT(r_["Bk"], r_["w"], -ck / 3, r_["Z"], M, Ad))
                    pool("Ea" if k < 2 else "Eb")
                    inc(STT(r_["M"], r_[es[k]], -pk * BETA, r_["Ea" if k < 2 else "Eb"], M, Ad))
                    mine(f"M{k + 1}")
                    inc(STT(r_[es[k + 1]], r_[names[k]], -pk, r_["M"], M, Ad))
                    dve.wait_ge(rk_pe, 4 * t + k + 1)
                    mine(f"B{k + 1}")
                    inc(STT(r_[names[k + 1]], a_of(k), ck, r_["Bk"], M, Ad))
                c4 = DT / 6
                mine("e4")
                inc(STT(r_["Z"], r_["e_d"], c4, r_["R"], M, Ad))
                pool("S2")
                inc(STT(r_["S3"], r_["e_d"], -(1 - A_P * BETA), r_["S2"], M, Ad))
                sq_done(3)
                inc(STT(r_["w"], r_["qsq"], -3.0 - 1 / c4, r_["q4"], Ad, M))
                mine("w4")
                inc(STT(r_["Bk"], r_["w"], -c4 / 3, r_["Z"], M, Ad))
                mine("S3")
                inc(STT(r_["S4"], r_["q4"], A_P, r_["S3"], M, Ad))
                mine("S4")
                inc(STT(r_["pr"], r_["S4"], 1 / 3, r_["h_row"], M, Ad))
                dve.wait_ge(rk_pe, 4 * t + 4)
                mine("B4")
                inc(STT(r_["qraw"], a_of(3), c4, r_["Bk"], M, Ad))
                mine("q_raw")
                inc(dve.tensor_scalar(r_["q"], r_["qraw"], CLAMP, -CLAMP, ALU.min, ALU.max))
                mine("p_raw")
                inc(dve.tensor_scalar(r_["p"], r_["pr"], CLAMP, -CLAMP, ALU.min, ALU.max))
                mine("p")
                inc(dve.tensor_tensor(r_["e_a"], r_["d_row"], r_["p"], ALU.subtract))

        @block.gpsimd
        def _(pool):
            start_counts(pool, "pool")
            TT, TS = pool.tensor_tensor, pool.tensor_scalar

            def modulate(buf, factors, which_scale, which_shift, g, s_dve, s_pool):
                pool.wait_ge(s_dve, 2 * g + 2)
                TT(buf[:, :, :], buf[:, :, :], factors[:, :].unsqueeze(1).to_broadcast([P, KC, GT]), ALU.mult).then_inc(s_pool, 1)
                pool.wait_ge(s_pool, 3 * g + 1)
                b4 = buf[:, :, :].rearrange("p c (b t) -> p c b t", t=T)
                for i, (which, op) in enumerate(((which_scale, ALU.mult), (which_shift, ALU.add))):
                    for c in range(KC):
                        r = TT(b4[:, c], b4[:, c], ada_rows(which, g, c), op)
                    r.then_inc(s_pool, 1)
                    if i == 0:
                        pool.wait_ge(s_pool, 3 * g + 2)

            pool.wait_ge(ada_dn, 1)
            modulate(xc, rs, SCALE1, SHIFT1, 0, ln_dve, ln_pool)
            n = 0

            def split(hi, lo, src):
                nonlocal n
                pool.wait_ge(ld_stage, 16 * (n + 1))
                TS(hi, src, 1.0, 0.0, ALU.mult, ALU.add).then_inc(pool_w, 1)
                pool.wait_ge(pool_w, 2 * n + 1)
                TT(lo, src, hi.bitcast(F32), ALU.subtract).then_inc(pool_w, 1)
                n += 1

            flat = stage[:, :, :].rearrange("p a b -> p (a b)")
            for u in range(1, NU + 1):
                for kc in range(KC if u < NU else 0):
                    split(W_hi[:, u, kc, :, :].rearrange("p a b -> p (a b)"),
                          W_lo[:, u, kc, :, :].rearrange("p a b -> p (a b)"), flat)
                hs = slice(HU * (u - 1), HU * u)
                split(wo_hi[:, hs, :].rearrange("p a b -> p (a b)"), wo_lo[:, hs, :].rearrange("p a b -> p (a b)"),
                      flat[:, 0:HU * D])

            with pool.Fori(1, NG) as g:
                modulate(xc, rs, SCALE1, SHIFT1, g, ln_dve, ln_pool)

            def finish(g):
                for c in range(KC):
                    pool.wait_ge(fgate, 1 + KC * g + c + 1)
                    TT(ysc[:, :], ysc[:, :], group(x_all, g, c), ALU.add).then_inc(ffn_out, 1)
                    if c == 0:
                        pool.wait_ge(ld_late, 96)
                    pool.wait_ge(ffn_out, 1 + 4 * g + 2 * c + 1)
                    dst = xtb[:, c, :, bass.ds(g * GB, GB)] if not isinstance(g, int) else xtb[:, c, :, g * GB:g * GB + GB]
                    TT(dst.rearrange("p t b -> p b t"), by_batch(ysc[:, :]), by_batch(group(xorig, g, c)),
                       ALU.add).then_inc(ffn_out, 1)

            modulate(fc, frs, SCALE2, SHIFT2, 0, l2_dve, l2_pool)
            with pool.Fori(0, NG - 1) as g:
                modulate(fc, frs, SCALE2, SHIFT2, g + 1, l2_dve, l2_pool)
                finish(g)
            finish(NG - 1)

            def split_inputs(j):
                t8, at8 = (slice(0, 8), slice(0, GT)) if isinstance(j, int) else (bass.ds(8 * j, 8), bass.ds(GT * j, GT))
                for c in range(KC):
                    r = pool.tensor_copy(y_hi[:, c, at8], xtb[:, c, t8, :].rearrange("p t b -> p (t b)"))
                r.then_inc(y_split, 1)
                pool.wait_ge(y_split, 2 * j + 1)
                TT(y_lo[:, :, at8], xtb[:, :, t8, :].rearrange("p c t b -> p c (t b)"), y_hi[:, :, at8].bitcast(F32),
                   ALU.subtract).then_inc(y_split, 1)

            def keep_state(t):
                pool.wait_ge(gru_dve, 1 + len(GRU_DVE) * t + len(GRU_DVE))
                xt = xtb[:, :, bass.ds(t, 1), :].rearrange("p c t b -> p c (t b)") if not isinstance(t, int) else xtb[:, :, t, :]
                TT(xt, xt, ht[:, :, :], ALU.add).then_inc(gru_out, 1)

            pool.wait_ge(ffn_out, 1 + 4 * NG)
            pool.wait_ge(down_done, 1 + KC * NG)
            split_inputs(0)
            with pool.Fori(0, NG - 1) as j:
                for s_ in range(8):
                    keep_state(8 * j + s_)
                    if s_ == 0:
                        split_inputs(j + 1)
            for s_ in range(8):
                keep_state(8 * (NG - 1) + s_)

            pool.wait_ge(gru_out, 1 + T)
            pool.memset(d_all[:, :, T, :], 0.0)
            pool.memset(g_all[:, :, T, :], 0.0)
            pool.memset(rk["third"][:, :, :], 1 / 3)
            for j in range(4):
                js = slice(8 * j, 8 * j + 8)
                pool.wait_ge(p_dve, 21 + 3 * j)

                def flatc(tile, c):
                    return tile[:, c, js, :].rearrange("p t b -> p (t b)")
                for c in range(KC):
                    r = TS(flatc(yt, c), flatc(yt, c), col("ln_gamma", c), col("ln_beta", c), ALU.mult, ALU.add)
                r.then_inc(p_pool, 1)
                pool.wait_ge(p_pool, 5 * j + 1)
                TT(xtb[:, :, js, :].rearrange("p c t b -> p c (t b)"), xtb[:, :, js, :].rearrange("p c t b -> p c (t b)"),
                   yt[:, :, js, :].rearrange("p c t b -> p c (t b)"), ALU.add).then_inc(p_pool, 1)
                pool.wait_ge(p_pool, 5 * j + 2)
                for c in range(KC):
                    r = TS(flatc(d_all, c), flatc(xtb, c), 1.0, col("l3_bias", c), ALU.mult, ALU.add)
                r.then_inc(p_pool, 1)
                pool.wait_ge(p_pool, 5 * j + 3)
                for c in range(KC):
                    TS(flatc(g_all, c), flatc(d_all, c), A_P * BETA, -A_P * ALPHA, ALU.mult, ALU.add)
                    r = TS(flatc(h_all, c), flatc(d_all, c), 1 - A_P * BETA / 3, A_P * ALPHA / 3, ALU.mult, ALU.add)
                r.then_inc(p_pool, 2)

            pool.wait_ge(rk0, 2)
            pool.wait_ge(p_pool, 20)
            r_ = {n: rk[n][:, :, :] for n in rk}
            pool.tensor_copy(r_["g_row"], g_all[:, :, 0, :]).then_inc(rk_pool, 1)
            with pool.Fori(0, T) as t:
                def at_step(tile, i):
                    return tile[:, :, bass.ds(i, 1), :].rearrange("p c t b -> p c (t b)")

                def dve_(name):
                    pool.wait_ge(rk_dve, RK_START + at(t, RK_DVE, name))

                def mine(name):
                    pool.wait_ge(rk_pool, 1 + at(t, RK_POOL, name))

                pool.wait_ge(rk_dve, RK_START + len(RK_DVE) * t)
                pool.wait_ge(rk_pool, 1 + len(RK_POOL) * t)
                TT(r_["Ea"], r_["e_a"], r_["g_row"], ALU.add).then_inc(rk_pool, 1)
                mine("Ea")
                TT(r_["Eb"], r_["Ea"], r_["g_row"], ALU.add).then_inc(rk_pool, 1)
                mine("Eb")
                pool.tensor_copy(r_["h_row"], at_step(h_all, t))
                pool.tensor_copy(r_["d_row"], at_step(d_all, t + 1))
                pool.tensor_copy(r_["g_row"], at_step(g_all, t + 1)).then_inc(rk_pool, 1)
                dve_("q2")
                TT(r_["R1"], r_["q2"], r_["q"], ALU.subtract).then_inc(rk_pool, 1)
                mine("R1")
                TT(r_["R1t"], r_["R1"], r_["third"], ALU.mult).then_inc(rk_pool, 1)
                TT(r_["S1"], r_["e_a"], r_["e_b"], ALU.subtract).then_inc(rk_pool, 1)
                dve_("e3")
                mine("S1")
                TT(r_["S1b"], r_["S1"], r_["e_c"], ALU.subtract).then_inc(rk_pool, 1)
                mine("S1b")
                TT(r_["S2"], r_["S1b"], r_["e_c"], ALU.subtract).then_inc(rk_pool, 1)
                xt = xtb[:, :, bass.ds(t, 1), :].rearrange("p c t b -> p c (t b)")
                dve_("q")
                TT(xt, xt, r_["q"], ALU.add).then_inc(rk_out, 1)


def _features(a):
    a = np.asarray(a)
    return np.moveaxis(a.reshape(-1, P, *a.shape[1:]), 0, 1)


def kernel(**inputs):
    import concourse.bacc as bacc
    from concourse.bass_utils import run_bass_kernel_spmd

    a = {k: np.asarray(v) for k, v in inputs.items()}
    qkv = a["L0_cond_qkv_w"].reshape(KC, P, 3, NU, HU * DH)
    arrays = {
        "xT": _features(a["x"].reshape(TOK, D).T),
        "cond": _features(a["cond_2048"].T),
        "ada_w": _features(a["L0_cond_ada_w"]),
        "qkv_w": qkv.transpose(3, 1, 0, 2, 4).reshape(NU, P, KC, 3 * HU * DH),
        "out_w": _features(a["L0_cond_out_w"]).reshape(P, HEADS * D),
        "ffn_w1": _features(a["L0_cond_ffn_w1"]),
        "ffn_w2": _features(a["L0_cond_ffn_w2"]),
        "w_ih": _features(a["L1_cond_W_ih"]),
        "w_hh": _features(a["L1_cond_W_hh"]),
        "wk": _features(a["L2_cond_Wk"].T),
        "wo": _features(a["L2_cond_Wo"].T),
        "coup": _features(a["L3_cond_coupling"].T),
        "vecs": np.concatenate([_features(a[n]) for n in (
            "L0_cond_ada_b", "L0_cond_qkv_b", "L0_cond_out_b", "L0_cond_ffn_b1", "L0_cond_ffn_b2", "L1_cond_b_ih",
            "L1_cond_b_hh", "L2_cond_rms_weight", "L2_cond_ln_gamma", "L2_cond_ln_beta", "L3_cond_bias")], axis=1),
    }
    arrays = {k: np.ascontiguousarray(v) for k, v in arrays.items()}
    nc = bacc.Bacc("TRN2", target_bir_lowering=False, num_devices=1)
    args = [nc.dram_tensor(k, v.shape, mybir.dt.from_np(v.dtype), kind="ExternalInput").ap() for k, v in arrays.items()]
    out = nc.dram_tensor("out", (P, KC, T, B), F32, kind="ExternalOutput").ap()
    build(nc, *args, out)
    r = run_bass_kernel_spmd(nc, [arrays], core_ids=[0])
    o = np.asarray(r.results[0]["out"])
    return np.ascontiguousarray(o.transpose(3, 2, 1, 0)).reshape(B, T, D)
```

```python
import numpy as np
import concourse.bass as bass
from concourse import mybir

F32 = mybir.dt.float32
F32R = mybir.dt.float32r
BF16 = mybir.dt.bfloat16
ACT = mybir.ActivationFunctionType
ALU = mybir.AluOpType
AX = mybir.AxisListType

P = 128
B, T, D = 64, 32, 256
KC = D // P
TOK = B * T
NG = 4
GT = TOK // NG
GB = B // NG
NT = GT // P
BT = P // T
HEADS, DH = 16, 128
NU = 4
HU = HEADS // NU
INNER = HEADS * DH
MLP = 4 * D
MC = MLP // P
NBLK, BLK = 8, T // 8
DT, EPSILON, ALPHA, BETA, CLAMP = 0.01, 0.08, 0.7, 0.8, 20.0
LN_EPS = 1e-6
A_P = EPSILON * DT / 2
WARM_GRU, WARM_RK = 28, 16

VEC = {}
_at = 0
for _name, _n in (("ada_b", 12), ("qkv_b", 48), ("out_b", 2), ("ffn_b1", 8), ("ffn_b2", 2), ("b_ih", 6),
                  ("b_hh", 6), ("rms_w", 2), ("ln_gamma", 2), ("ln_beta", 2), ("l3_bias", 2)):
    VEC[_name] = _at
    _at += _n
NVEC = _at
SHIFT1, SCALE1, GATE1, SHIFT2, SCALE2, GATE2 = range(6)

SOFT = ("max", "sub", "sum", "recip", "norm", "tr0", "tr1", "tr2", "tr3")
GATE = ("gate0", "add0", "gate1", "add1")
GRU_DVE = ("pre_r", "r_bias", "n_base", "pre_z", "r_hn", "pre_n", "z_h", "zc_n", "h")
GRU_ACT = ("r", "z", "zc", "n")
GRU_PE = ("r", "z", "hn")
RK_ACT = ("tanh", "square")
RK_DVE = ("Z1", "w1", "B1", "M1", "e2", "q2",
          "Z2", "w2", "B2", "M2", "e3", "q3",
          "Z3", "w3", "R", "B3", "M3", "e4", "q4",
          "Z4", "S3", "w4", "B4", "S4", "p_raw", "q_raw", "q", "p", "e1")
RK_POOL = ("Ea", "Eb", "h_row", "R1", "R1t", "d_row", "S1", "S1b", "g_row", "S2")
POOL_DVE = ("score_vec", "wo_sum", "wqr", "keys0", "keys1", "wo_mean", "wo_c", "rms_inv", "score", "score_max", "score_sub",
            "sum", "recip", "att_mul0", "att_sum0", "att0", "att_mul1", "att_sum1", "att1")
RK_START = 3


def at(step, events, name):
    return step * len(events) + events.index(name) + 1


def build(nc, xT, cond, ada_w, qkv_w, out_w, ffn_w1, ffn_w2, w_ih, w_hh, wk, wo, coup, vecs, out):
    from contextlib import ExitStack

    ctx = ExitStack()
    base = (nc.sbuf_base + 127) // 128 * 128
    end = nc.sbuf_usable_end
    KB = 1024

    def place(name, shape, dtype, offset):
        size = (int(np.prod(shape[1:])) * (2 if dtype == BF16 else 4) + 31) // 32 * 32
        assert offset + size <= end, (name, offset + size, end)
        return nc.alloc_sbuf_tensor_at(name, shape, dtype, offset=offset), offset + size

    def row(at_, *tiles):
        made = []
        for name, shape, dtype in tiles:
            t, at_ = place(name, shape, dtype, at_)
            made.append(t)
        return (*made, at_)

    with ctx:
        x_all, ada, vec, cnd, ones, eps_t, gb, idle, perm = row(
            base, ("x_all", [P, KC, TOK], F32), ("ada", [P, 12, B], F32), ("vec", [P, NVEC], F32),
            ("cnd", [P, KC, B], F32), ("ones", [P, P], F32),
            ("eps_t", [P, 8], F32), ("gb", [P, 8], F32), ("idle", [P, P], BF16))
        W_hi, W_lo, a_w = row(perm, ("W_hi", [P, NU, KC, 3, HU * DH], F32R), ("W_lo", [P, NU, KC, 3, HU * DH], F32R))
        (wo_hi, wo_lo, stage, xc, sq, rs, x_hi, x_lo, qk, V, Pr, BD, o_hi, o_lo, mx, sm, a_end) = row(
            a_w, ("wo_hi", [P, HEADS, D], F32R), ("wo_lo", [P, HEADS, D], F32R), ("stage", [P, 3, HU * DH], F32),
            ("xc", [P, KC, GT], F32), ("sq", [P, KC, GT], F32), ("rs", [P, GT], F32),
            ("x_hi", [P, KC, GT], F32R), ("x_lo", [P, KC, GT], F32R),
            ("qk", [P, 2, 2, GT], F32), ("V", [P, NT, HU * DH], F32), ("Pr", [P, NT * HU, T], F32),
            ("BD", [P, NT * HU, P], F32), ("o_hi", [P, 2, GT], F32R), ("o_lo", [P, 2, GT], F32R),
            ("mx", [P, NT * HU], F32), ("sm", [P, NT * HU], F32))
        q_off = perm + 2 * 48 * KB + 32 * KB + 6 * KB + 4 * KB * 2 + 2 * KB + 8 * KB
        ada_sb, _ = place("ada_sb", [P, KC, 6 * D], F32, q_off)
        (f1_raw, f2_raw, f1_hi, f1_lo, f2_hi, f2_lo, m_hi, m_lo, g_hi, g_lo, f_w) = row(
            perm, ("f1_raw", [P, KC, MLP], F32), ("f2_raw", [P, MC, D], F32),
            ("f1_hi", [P, KC, MLP], F32R), ("f1_lo", [P, KC, MLP], F32R),
            ("f2_hi", [P, MC, D], F32R), ("f2_lo", [P, MC, D], F32R),
            ("m_hi", [P, KC, GT], F32R), ("m_lo", [P, KC, GT], F32R),
            ("g_hi", [P, MC, GT], F32R), ("g_lo", [P, MC, GT], F32R))
        assert f_w <= a_w
        (xtb, xtb_end) = row(a_w, ("xtb", [P, KC, T + 1, B], F32))
        (xorig, fc, fsq, frs, gel, ysc, ih_raw, hh, ih_hi, ih_lo, wk_sb, wo_sb, cp, blk, blk_part, f_end) = row(
            xtb_end, ("xorig", [P, KC, TOK], F32), ("fc", [P, KC, GT], F32),
            ("fsq", [P, KC, GT], F32), ("frs", [P, GT], F32), ("gel", [P, 2, GT], F32), ("ysc", [P, GT], F32),
            ("ih_raw", [P, KC, 3 * D], F32), ("hh", [P, KC, 3 * D], F32),
            ("ih_hi", [P, KC, 3 * D], F32R), ("ih_lo", [P, KC, 3 * D], F32R),
            ("wk_sb", [P, KC, D], F32), ("wo_sb", [P, KC, D], F32), ("cp", [P, KC, D], F32),
            ("blk", [P, KC, NBLK, B], F32), ("blk_part", [P, KC, B], F32))
        (gi, y_hi, y_lo, ht, ar, az, rg, zg, zcg, ng, rb, nb, zh, rn, pn, zn, bhn, g_end) = row(
            perm, ("gi", [P, 6, T, B], F32), ("y_hi", [P, KC, TOK], F32R), ("y_lo", [P, KC, TOK], F32R),
            ("ht", [P, KC, B], F32), *[(n, [P, KC, B], F32) for n in (
                "ar", "az", "rg", "zg", "zcg", "ng", "rb", "nb", "zh", "rn", "pn", "zn", "bhn")])
        (yt, yt2, frs4, keys, keys2, wqr, s_rs, s_sc, s_at, s_mx, s_wb, att, wo_c, wo_m, l_end) = row(
            perm, ("yt", [P, KC, T, B], F32), ("yt2", [P, KC, T, B], F32), ("frs4", [P, T, B], F32),
            ("keys", [P, KC, NBLK * B], F32), ("keys2", [P, KC, NBLK * B], F32),
            ("wqr", [P, KC, P], F32), ("s_rs", [P, NBLK * B], F32), ("s_sc", [P, NBLK, B], F32),
            ("s_at", [P, NBLK, B], F32), ("s_mx", [P, 2, B], F32), ("s_wb", [P, NBLK, B], F32),
            ("att", [P, KC, B], F32), ("wo_c", [P, KC, D], F32), ("wo_m", [P, KC], F32))
        assert g_end <= a_w and l_end <= a_w
        RKN = ("q", "th", "qsq", "w", "Bk", "Z", "e_a", "e_b", "e_c", "e_d", "M", "Ea", "Eb", "R1", "R",
               "R1t", "S1", "S1b", "S2", "S3", "S4", "pr", "p", "third", "g_row", "h_row", "d_row", "qraw", "q2", "q3", "q4")
        rk = {}
        off = xtb_end
        for n in RKN:
            rk[n], off = place("rk_" + n, [P, KC, B], F32, off)
        assert off <= xtb_end + 16 * KB

        ps = ctx.enter_context(nc.psum_tensor("ps", [P, 8, 512], F32))
        PJ = (0, 1)
        SB = 2
        OB = (3, 4)
        YB = (5, 6)
        TB = 7
        MEAN_BANK, VAR_BANK = (*YB, *PJ), (OB[0], SB, *YB)

        def sem(name):
            return ctx.enter_context(nc.semaphore(name))

        ld_x, ld_x0, ld_v, ld_ada = sem("ld_x"), sem("ld_x0"), sem("ld_v"), sem("ld_ada")
        ld_w = [sem(f"ld_w{i}") for i in range(2)]
        ld_ffn = [sem(f"ld_ffn{i}") for i in range(2)]
        ld_stage, ld_late = sem("ld_stage"), sem("ld_late")
        consts, ada_mm, ada_dn, w_hi0, w_rdy, pool_w, wo_rdy = (sem(n) for n in (
            "consts", "ada_mm", "ada_dn", "w_hi0", "w_rdy", "pool_w", "wo_rdy"))
        ln_pe, ln_dve, ln_act, ln_pool, x1_hi, x1_lo = (sem(n) for n in (
            "ln_pe", "ln_dve", "ln_act", "ln_pool", "x1_hi", "x1_lo"))
        proj_done, act_evac, dve_evac, scores_done, soft, exp_done = (sem(n) for n in (
            "proj_done", "act_evac", "dve_evac", "scores_done", "soft", "exp_done"))
        pv_done, ohi_done, olo_done, out_done, gate_done = (sem(n) for n in (
            "pv_done", "ohi_done", "olo_done", "out_done", "gate_done"))
        l2_pe, l2_dve, l2_act, l2_pool, m_hi_s, m_lo_s, fw_hi, fw_lo = (sem(n) for n in (
            "l2_pe", "l2_dve", "l2_act", "l2_pool", "m_hi_s", "m_lo_s", "fw_hi", "fw_lo"))
        up_done, gel_done, glo_done, down_done, fgate, ffn_out = (sem(n) for n in (
            "up_done", "gel_done", "glo_done", "down_done", "fgate", "ffn_out"))
        iw_hi, iw_lo, y0_hi, y_split, gi_mm, gi_act = (sem(n) for n in (
            "iw_hi", "iw_lo", "y0_hi", "y_split", "gi_mm", "gi_act"))
        h0, gru_pe, gru_act, gru_dve, gru_out = (sem(n) for n in ("h0", "gru_pe", "gru_act", "gru_dve", "gru_out"))
        p_pe, p_dve, p_act, p_keys, p_mean, p_cen, p_y, p_sq, p_var, p_dev, p_inv, p_norm, p_norm3, p_aff, p_add, blk_done, blk_turn = (
            sem(n) for n in ("p_pe", "p_dve", "p_act", "p_keys", "p_mean", "p_cen", "p_y", "p_sq", "p_var", "p_dev", "p_inv",
                             "p_norm", "p_norm3", "p_aff", "p_add", "blk_done", "blk_turn"))
        rk_pe, rk_act, rk_dve, rk_pool, rk_out, rk0, stored = (sem(n) for n in (
            "rk_pe", "rk_act", "rk_dve", "rk_pool", "rk_out", "rk0", "stored"))

        def col(name, i):
            return vec[:, VEC[name] + i:VEC[name] + i + 1]

        def ada_rows(which, g, c=None):
            lo = 2 * which
            bs = bass.ds(g * GB, GB) if not isinstance(g, int) else slice(g * GB, g * GB + GB)
            if c is not None:
                return ada[:, lo + c, bs].unsqueeze(2).to_broadcast([P, GB, T])
            return ada[:, lo:lo + 2, bs].unsqueeze(3).to_broadcast([P, KC, GB, T])

        def group(tile, g, c=None):
            ts = bass.ds(g * GT, GT) if not isinstance(g, int) else slice(g * GT, g * GT + GT)
            return tile[:, :, ts] if c is None else tile[:, c, ts]

        def by_batch(ap):
            return ap.rearrange("p (b t) -> p b t", t=T)

        def quarter(tile, j, c=None):
            rows = tile[:, :, 8 * j:8 * j + 8, :]
            return rows.rearrange("p c t b -> p c (t b)") if c is None else rows[:, c].rearrange("p t b -> p (t b)")

        def by_row(tile, j):
            return tile[:, 8 * j:8 * j + 8, :].rearrange("p t b -> p (t b)").unsqueeze(1).to_broadcast([P, KC, GT])

        counts_from_one = {"pe": (pv_done, out_done, down_done, gi_mm),
                           "act": (gel_done, gi_act),
                           "dve": (olo_done, gate_done, glo_done, fgate, gru_dve, rk_dve),
                           "pool": (ffn_out, gru_out, rk_out)}

        def start_counts(engine, name):
            for s in counts_from_one[name]:
                engine.sem_inc(s, RK_START if s is rk_dve else 1)

        block = ctx.enter_context(nc.Block())

        @block.sync
        def _(sp):
            sp.dma_start(vec[:, :], vecs).then_inc(ld_v, 16)
            sp.dma_start(cnd[:, :, :], cond).then_inc(ld_v, 16)
            sp.dma_start(x_all[:, :, 0:GT], xT[:, :, 0:GT]).then_inc(ld_x0, 16)
            sp.dma_start(ada_sb[:, :, :], ada_w).then_inc(ld_ada, 16)
            sp.dma_start(BD[:, 0:12, :].rearrange("p a b -> p (a b)"), qkv_w[0, :, 0, :]).then_inc(ld_w[0], 16)
            sp.dma_start(stage[:, :, :].rearrange("p a b -> p (a b)"), qkv_w[0, :, 1, :]).then_inc(ld_w[1], 16)
            sp.dma_start(x_all[:, :, GT:TOK], xT[:, :, GT:TOK]).then_inc(ld_x, 16)
            n = 0
            for u in range(1, NU + 1):
                for kc in range(KC if u < NU else 0):
                    if n == 0:
                        sp.wait_ge(w_rdy, 2)
                    else:
                        sp.wait_ge(pool_w, 2 * n)
                    sp.dma_start(stage[:, :, :].rearrange("p a b -> p (a b)"),
                                 qkv_w[u, :, kc, :]).then_inc(ld_stage, 16)
                    n += 1
                sp.wait_ge(pool_w, 2 * n)
                sp.dma_start(stage[:, 0:2, :].rearrange("p a b -> p (a b)"),
                             out_w[:, HU * (u - 1) * D:HU * u * D]).then_inc(ld_stage, 16)
                n += 1
            sp.wait_ge(proj_done, 12 * NU * NG)
            sp.dma_start(f1_raw[:, :, :], ffn_w1).then_inc(ld_ffn[0], 16)
            sp.dma_start(f2_raw[:, :, :], ffn_w2).then_inc(ld_ffn[1], 16)
            sp.wait_ge(gate_done, 1 + len(GATE) * NG)
            sp.wait_ge(out_done, 1 + HEADS * NG)
            sp.dma_start(xorig[:, :, :], xT).then_inc(ld_late, 16)
            sp.dma_start(ih_raw[:, :, :], w_ih).then_inc(ld_late, 16)
            sp.dma_start(hh[:, :, :], w_hh).then_inc(ld_late, 16)
            sp.dma_start(wk_sb[:, :, :], wk).then_inc(ld_late, 16)
            sp.dma_start(wo_sb[:, :, :], wo).then_inc(ld_late, 16)
            sp.dma_start(cp[:, :, :], coup).then_inc(ld_late, 16)
            for i in range(4):
                sp.wait_ge(rk_out, 1 + 8 * (i + 1))
                sp.dma_start(out[:, :, 8 * i:8 * i + 8, :], xtb[:, :, 8 * i:8 * i + 8, :]).then_inc(stored, 16)
            sp.wait_ge(stored, 64)

        @block.tensor
        def _(pe):
            start_counts(pe, "pe")

            def three(out_, pairs, first=True, last=True):
                n = 3 * len(pairs)
                i = 0
                for lh, ll, rh, rl in pairs:
                    for lhsT, rhs in ((lh, rh), (ll, rh), (lh, rl)):
                        r = pe.matmul(out_, lhsT, rhs, start=first and i == 0, stop=last and i == n - 1)
                        i += 1
                return r

            def stat(src, s):
                for c in range(KC):
                    r = pe.matmul(ps[:, TB, :], ones[:, :], src[c], start=c == 0, stop=c == KC - 1)
                r.then_inc(s, 1)

            def ln_mean(g):
                if not isinstance(g, int) or g:
                    pe.wait_ge(ln_act, 2 * g)
                    pe.wait_ge(ld_x, 16)
                else:
                    pe.wait_ge(ld_x0, 16)
                stat([group(x_all, g, c) for c in range(KC)], ln_pe)

            def ln_var(g):
                pe.wait_ge(ln_act, 2 * g + 1)
                stat([sq[:, c, :] for c in range(KC)], ln_pe)

            def proj(n, ng, u, piece):
                kind, i = piece
                p = {"q": 2 * i, "k": 2 * i + 1, "v": 8 + i}[kind]
                if p == 0:
                    if u == 0:
                        pe.wait_ge(x1_lo, ng + 1)
                        pe.wait_ge(w_rdy, 2)
                    else:
                        pe.wait_ge(pool_w, 6 * u - 2)
                if p >= 2 or not (isinstance(n, int) and n == 0):
                    pe.wait_ge(act_evac if p % 2 == 0 else dve_evac, 6 * n + p // 2)
                o = ps[:, PJ[p % 2], :]
                if kind == "v":
                    ts = slice(i * P, i * P + P)
                    r = three(o, [(x_hi[:, c, ts], x_lo[:, c, ts], W_hi[:, u, c, 2, :], W_lo[:, u, c, 2, :])
                                  for c in range(KC)])
                else:
                    t, hs = "qk".index(kind), slice(i * DH, i * DH + DH)
                    r = three(o, [(W_hi[:, u, c, t, hs], W_lo[:, u, c, t, hs], x_hi[:, c, :], x_lo[:, c, :])
                                  for c in range(KC)])
                r.then_inc(proj_done, 1)

            def scores(n, h):
                pe.wait_ge(act_evac, 6 * n + h + 1)
                pe.wait_ge(dve_evac, 6 * n + h + 1)
                if h == 0 and not (isinstance(n, int) and n == 0):
                    pe.wait_ge(soft, len(SOFT) * (n - 1) + 2)
                for i in range(NT):
                    for j in range(BT):
                        t = slice(i * P + j * T, i * P + j * T + T)
                        r = pe.matmul(ps[j * T:j * T + T, SB, (i * HU + h) * T:(i * HU + h) * T + T],
                                      qk[:, 0, h % 2, t], qk[:, 1, h % 2, t], start=True, stop=True)
                r.then_inc(scores_done, 1)

            def pv(U, h):
                if h == 0:
                    pe.wait_ge(soft, len(SOFT) * (U + 1))
                    pe.wait_ge(act_evac, 6 * (U + 1))
                    pe.wait_ge(dve_evac, 6 * (U + 1))
                pe.wait_ge(olo_done, 1 + 4 * U + max(h - 1, 0))
                for i in range(NT):
                    r = pe.matmul(ps[:, OB[h % 2], i * P:i * P + P], V[:, i, h * DH:h * DH + DH],
                                  BD[:, i * HU + h, :], start=True, stop=True)
                r.then_inc(pv_done, 1)

            def head_sum(U, u, h, g):
                pe.wait_ge(olo_done, 1 + 4 * U + h + 1)
                if h == 0:
                    pe.wait_ge(pool_w, 6 * (u + 1) if u < 3 else 20)
                    if u == 0:
                        pe.wait_ge(gate_done, 1 + len(GATE) * g)
                k = HU * u + h
                for c in range(KC):
                    cs = slice(c * P, c * P + P)
                    r = three(ps[:, YB[c], :], [(wo_hi[:, k, cs], wo_lo[:, k, cs], o_hi[:, h % 2, :], o_lo[:, h % 2, :])],
                              first=k == 0, last=k == HEADS - 1)
                r.then_inc(out_done, 1)

            pe.wait_ge(consts, 1)
            ln_mean(0)
            pe.wait_ge(ld_v, 32)
            pe.wait_ge(ld_ada, 16)
            for j in range(12):
                for c in range(KC):
                    r = pe.matmul(ps[:, YB[j // 6], (j % 6) * B:(j % 6) * B + B], ada_sb[:, c, j * P:j * P + P],
                                  cnd[:, c, :], start=c == 0, stop=c == KC - 1)
            r.then_inc(ada_mm, 1)
            ln_var(0)

            FIRST = [("q", 0), ("k", 0), ("q", 1), ("k", 1), ("S", 0), ("q", 2), ("k", 2), ("S", 1), ("q", 3), ("k", 3),
                     ("S", 2), ("v", 0), ("S", 3), ("v", 1), ("v", 2), ("v", 3)]
            STEP = [("q", 0), ("k", 0), ("q", 1), ("k", 1), ("S", 0), ("q", 2), ("k", 2), ("S", 1), ("PV", 0), ("q", 3),
                    ("PV", 1), ("k", 3), ("Y", 0), ("S", 2), ("PV", 2), ("Y", 1), ("PV", 3), ("S", 3), ("v", 0),
                    ("Y", 2), ("v", 1), ("v", 2), ("v", 3), ("Y", 3)]

            def run(order, U, u, g, project):
                n = U + 1 if U is not None else 0
                ng = 0 if U is None else g if u < NU - 1 else g + 1
                un = (u + 1) % NU if U is not None else 0
                for kind, i in order:
                    if kind == "PV":
                        pv(U, i)
                    elif kind == "Y":
                        head_sum(U, u, i, g)
                    elif not project:
                        pass
                    elif kind == "S":
                        scores(n, i)
                    else:
                        proj(n, ng, un, (kind, i))

            run(FIRST, None, 0, 0, True)

            def l2_mean(g):
                pe.wait_ge(gate_done, 1 + len(GATE) * (g + 1))
                if not isinstance(g, int) or g:
                    pe.wait_ge(l2_act, 2 * g)
                else:
                    pe.wait_ge(ln_act, 2 * NG)
                stat([group(x_all, g, c) for c in range(KC)], l2_pe)

            def l2_var(g):
                pe.wait_ge(l2_act, 2 * g + 1)
                stat([(fsq if not isinstance(g, int) or g else sq)[:, c, :] for c in range(KC)], l2_pe)

            def attention(g, last):
                for u in range(NU):
                    U = NU * g + u
                    if not last and u == 0:
                        ln_mean(g + 1)
                    if not last and u == 1:
                        ln_var(g + 1)
                    if last and u == 1:
                        l2_mean(0)
                    if last and u == 2:
                        l2_var(0)
                    run(STEP, U, u, g, not (last and u == NU - 1))

            with pe.Fori(0, NG - 1) as g:
                attention(g, False)
            attention(NG - 1, True)

            def ffn(g, last):
                pe.wait_ge(m_lo_s, g + 1)
                for m in range(MC):
                    if not last and m == 0:
                        l2_mean(g + 1)
                    if not last and m == 4:
                        l2_var(g + 1)
                    pe.wait_ge(gel_done, 1 + 2 * (MC * g + max(m - 1, 0)))
                    ms = slice(m * P, m * P + P)
                    three(ps[:, PJ[m % 2], :], [(f1_hi[:, c, ms], f1_lo[:, c, ms], m_hi[:, c, :], m_lo[:, c, :])
                                                for c in range(KC)]).then_inc(up_done, 1)
                for c in range(KC):
                    pe.wait_ge(fgate, 1 + KC * g)
                    pe.wait_ge(gate_done, 1 + len(GATE) * NG)
                    pe.wait_ge(fw_lo, 2)
                    cs = slice(c * P, c * P + P)
                    for m in range(MC):
                        if c == 0:
                            pe.wait_ge(glo_done, 1 + MC * g + m + 1)
                        r = three(ps[:, YB[c], :], [(f2_hi[:, m, cs], f2_lo[:, m, cs], g_hi[:, m, :], g_lo[:, m, :])],
                                  first=m == 0, last=m == MC - 1)
                    r.then_inc(down_done, 1)

            pe.wait_ge(fw_lo, 1)
            with pe.Fori(0, NG - 1) as g:
                ffn(g, False)
            ffn(NG - 1, True)

            def keep_warm(n):
                for _ in range(n):
                    pe.matmul(ps[:, TB, 0:P], idle[:, :], idle[:, :], start=True, stop=True)

            def input_gates(j, m):
                if m == 0:
                    pe.wait_ge(y_split, 2 * j + 2)
                pe.wait_ge(gi_act, 1 + 6 * j + max(m - 1, 0))
                ms = slice(m * P, m * P + P)
                js = slice(0, GT) if isinstance(j, int) and j == 0 else bass.ds(GT * j, GT)
                three(ps[:, PJ[m % 2], :], [(ih_hi[:, c, ms], ih_lo[:, c, ms], y_hi[:, c, js], y_lo[:, c, js])
                                            for c in range(KC)]).then_inc(gi_mm, 1)

            def recur(t, j, s_, last):
                pe.wait_ge(gru_dve, 1 + len(GRU_DVE) * t)
                for part, bank in ((0, SB), (1, OB[0]), (2, OB[1])):
                    for c in range(KC):
                        ms = slice((KC * part + c) * P, (KC * part + c) * P + P)
                        for k in range(KC):
                            r = pe.matmul(ps[:, bank, c * B:c * B + B], hh[:, k, ms], ht[:, k, :],
                                          start=k == 0, stop=k == KC - 1)
                    r.then_inc(gru_pe, 1)
                if not last and s_ >= 2:
                    input_gates(j + 1, s_ - 2)
                else:
                    keep_warm(WARM_GRU)

            pe.wait_ge(iw_lo, 1)
            for m in range(6):
                input_gates(0, m)
            pe.wait_ge(h0, 1)
            with pe.Fori(0, NG - 1) as j:
                for s_ in range(8):
                    recur(8 * j + s_, j, s_, False)
            for s_ in range(8):
                recur(8 * (NG - 1) + s_, NG - 1, s_, True)

            def keys_mm(c):
                for k in range(KC):
                    r = pe.matmul(ps[:, PJ[c], :], wk_sb[:, k, c * P:c * P + P], blk[:, k, :, :].rearrange("p n b -> p (n b)"),
                                  start=k == 0, stop=k == KC - 1)
                r.then_inc(p_keys, 1)

            def mean_mm(j, bank):
                for c in range(KC):
                    r = pe.matmul(ps[:, bank, :], ones[:, :], xtb[:, c, 8 * j:8 * j + 8, :].rearrange("p t b -> p (t b)"),
                                  start=c == 0, stop=c == KC - 1)
                r.then_inc(p_mean, 1)

            pe.wait_ge(blk_done, 3 * NBLK)
            keys_mm(0)
            keys_mm(1)
            mean_mm(0, MEAN_BANK[0])
            mean_mm(1, MEAN_BANK[1])
            for k in range(KC):
                pe.wait_ge(p_dve, at(0, POOL_DVE, f"keys{k}"))
                r = pe.matmul(ps[:, SB, :], wqr[:, k, :], keys[:, k, :], start=k == 0, stop=k == KC - 1)
            r.then_inc(p_pe, 1)
            for k in range(KC):
                pe.wait_ge(p_act, k + 1)
                r = pe.matmul(ps[:, OB[0], :], ones[:, :], keys2[:, k, :], start=k == 0, stop=k == KC - 1)
            r.then_inc(p_pe, 1)
            mean_mm(2, MEAN_BANK[2])
            mean_mm(3, MEAN_BANK[3])
            keep_warm(40)
            pe.wait_ge(p_dve, at(0, POOL_DVE, "att1"))
            for c in range(KC):
                for k in range(KC):
                    r = pe.matmul(ps[:, OB[1], c * B:c * B + B], wo_c[:, k, c * P:c * P + P], att[:, k, :],
                                  start=k == 0, stop=k == KC - 1)
            r.then_inc(p_pe, 1)
            for j in range(4):
                pe.wait_ge(p_sq, j + 1)
                for c in range(KC):
                    r = pe.matmul(ps[:, VAR_BANK[j], :], ones[:, :],
                                  yt2[:, c, 8 * j:8 * j + 8, :].rearrange("p t b -> p (t b)"),
                                  start=c == 0, stop=c == KC - 1)
                r.then_inc(p_var, 1)

            pe.wait_ge(rk0, 2)
            with pe.Fori(0, T) as t:
                for k in range(4):
                    pe.wait_ge(rk_act, 8 * t + 2 * k + 1)
                    for c in range(KC):
                        for kk in range(KC):
                            r = pe.matmul(ps[:, SB if k % 2 == 0 else OB[0], c * B:c * B + B], cp[:, kk, c * P:c * P + P],
                                          rk["th"][:, kk, :], start=kk == 0, stop=kk == KC - 1)
                    r.then_inc(rk_pe, 1)
                    keep_warm(WARM_RK)

        @block.scalar
        def _(act):
            start_counts(act, "act")

            def ln_square(g):
                act.wait_ge(ln_dve, 2 * g + 1)
                if not isinstance(g, int) or g:
                    act.wait_ge(ln_pe, 2 * g)
                act.activation(sq[:, :, :], xc[:, :, :], ACT.Square).then_inc(ln_act, 1)

            def ln_sqrt(g):
                act.wait_ge(ln_pe, 2 * g + 2)
                if not isinstance(g, int) or g:
                    act.wait_ge(ln_pool, 3 * g)
                act.activation(rs[:, :], ps[:, TB, :], ACT.Sqrt, bias=eps_t[:, 0:1]).then_inc(ln_act, 1)

            def high(g):
                act.wait_ge(ln_pool, 3 * g + 3)
                if not isinstance(g, int) or g:
                    act.wait_ge(proj_done, 48 * g)
                act.activation(x_hi[:, :, :], xc[:, :, :], ACT.Copy).then_inc(x1_hi, 1)

            def query(n, u, h):
                act.wait_ge(proj_done, 12 * n + 2 * h + 1)
                if h >= 2 or not (isinstance(n, int) and n == 0):
                    act.wait_ge(scores_done, 4 * n + h - 1)
                else:
                    act.wait_ge(ada_mm, 1)
                act.activation(qk[:, 0, h % 2, :], ps[:, PJ[0], :], ACT.Identity,
                               bias=col("qkv_b", HU * u + h)).then_inc(act_evac, 1)

            def value(n, i):
                act.wait_ge(proj_done, 12 * n + 8 + i + 1)
                if not (isinstance(n, int) and n == 0):
                    act.wait_ge(pv_done, 1 + 4 * n)
                act.activation(V[:, i, :], ps[:, PJ[0], :], ACT.Copy).then_inc(act_evac, 1)

            def exp(U):
                act.wait_ge(soft, len(SOFT) * U + 2)
                act.activation(Pr[:, :, :], Pr[:, :, :], ACT.Exp, scale=DH ** -0.5).then_inc(exp_done, 1)

            def out_high(U, u, h):
                act.wait_ge(pv_done, 1 + 4 * U + h + 1)
                act.wait_ge(out_done, 1 + 4 * U + max(h - 1, 0))
                act.activation(o_hi[:, h % 2, :], ps[:, OB[h % 2], :], ACT.Identity,
                               bias=col("qkv_b", 2 * HEADS + HU * u + h)).then_inc(ohi_done, 1)

            act.wait_ge(consts, 1)
            ln_square(0)
            ln_sqrt(0)
            for kc, src in enumerate((BD[:, 0:12, :].rearrange("p a b -> p (a b)"),
                                      stage[:, :, :].rearrange("p a b -> p (a b)"))):
                act.wait_ge(ld_w[kc], 16)
                act.activation(W_hi[:, 0, kc, :, :].rearrange("p a b -> p (a b)"), src, ACT.Copy).then_inc(w_hi0, 1)
            high(0)
            for h in range(HU):
                query(0, 0, h)
            value(0, 0)
            value(0, 2)

            def l2_square(g):
                act.wait_ge(l2_dve, 2 * g + 1)
                if not isinstance(g, int) or g:
                    act.wait_ge(l2_pe, 2 * g)
                first = isinstance(g, int) and g == 0
                act.activation((sq if first else fsq)[:, :, :], (xc if first else fc)[:, :, :], ACT.Square).then_inc(l2_act, 1)

            def l2_sqrt(g):
                act.wait_ge(l2_pe, 2 * g + 2)
                if not isinstance(g, int) or g:
                    act.wait_ge(l2_pool, 3 * g)
                act.activation((rs if isinstance(g, int) and g == 0 else frs)[:, :], ps[:, TB, :], ACT.Sqrt, bias=eps_t[:, 0:1]).then_inc(l2_act, 1)

            def m_high(g):
                act.wait_ge(l2_pool, 3 * g + 3)
                if not isinstance(g, int) or g:
                    act.wait_ge(up_done, MC * g)
                else:
                    act.wait_ge(proj_done, 12 * NU * NG)
                act.activation(m_hi[:, :, :], (xc if isinstance(g, int) and g == 0 else fc)[:, :, :], ACT.Copy).then_inc(m_hi_s, 1)

            def attention(g, last):
                for u in range(NU):
                    U = NU * g + u
                    n, un = U + 1, (u + 1) % NU
                    project = not (last and u == NU - 1)
                    if u == NU - 1 and not last:
                        high(g + 1)
                    if project:
                        query(n, un, 0)
                    exp(U)
                    if project:
                        query(n, un, 1)
                    if u == 0 and not last:
                        ln_square(g + 1)
                    if u == 1 and not last:
                        ln_sqrt(g + 1)
                    if u == 1 and last:
                        l2_square(0)
                    if u == 2 and last:
                        l2_sqrt(0)
                    if u == NU - 1 and last:
                        m_high(0)
                    if project:
                        query(n, un, 2)
                    out_high(U, u, 0)
                    if project:
                        query(n, un, 3)
                    for h in range(1, HU):
                        out_high(U, u, h)
                    if project:
                        value(n, 0)
                        value(n, 2)

            with act.Fori(0, NG - 1) as g:
                attention(g, False)
            attention(NG - 1, True)

            def ffn(g, last):
                for m in range(MC):
                    act.wait_ge(up_done, MC * g + m + 1)
                    act.wait_ge(glo_done, 1 + MC * g + max(m - 1, 0))
                    act.activation(gel[:, m % 2, :], ps[:, PJ[m % 2], :], ACT.Gelu,
                                   bias=col("ffn_b1", m)).then_inc(gel_done, 1)
                    act.wait_ge(down_done, 1 + KC * g)
                    act.activation(g_hi[:, m, :], ps[:, PJ[m % 2], :], ACT.Gelu,
                                   bias=col("ffn_b1", m)).then_inc(gel_done, 1)
                    if m == 1 and not last:
                        l2_square(g + 1)
                    if m == 5 and not last:
                        l2_sqrt(g + 1)
                if not last:
                    m_high(g + 1)

            act.wait_ge(ld_ffn[0], 16)
            act.activation(f1_hi[:, :, :], f1_raw[:, :, :], ACT.Copy).then_inc(fw_hi, 1)
            act.wait_ge(ld_ffn[1], 16)
            act.activation(f2_hi[:, :, :], f2_raw[:, :, :], ACT.Copy).then_inc(fw_hi, 1)
            with act.Fori(0, NG - 1) as g:
                ffn(g, False)
            ffn(NG - 1, True)

            act.wait_ge(ld_late, 96)
            act.activation(ih_hi[:, :, :], ih_raw[:, :, :], ACT.Copy).then_inc(iw_hi, 1)
            act.wait_ge(down_done, 1 + KC * NG)
            for c in range(KC):
                act.wait_ge(ffn_out, 1 + 4 * (NG - 1) + 2 * c + 2)
                act.activation(y_hi[:, c, 0:GT], quarter(xtb, 0, c), ACT.Copy).then_inc(y0_hi, 1)
            act.wait_ge(h0, 1)

            def gates_out(j, m):
                act.wait_ge(gi_mm, 1 + 6 * j + m + 1)
                ts = slice(0, 8) if isinstance(j, int) and j == 0 else bass.ds(8 * j, 8)
                act.activation(gi[:, m, ts, :].rearrange("p t b -> p (t b)"), ps[:, PJ[m % 2], :],
                               ACT.Identity, bias=gb[:, m:m + 1]).then_inc(gi_act, 1)

            for m in range(6):
                gates_out(0, m)

            def recur(t, j, s_, last):
                def wait_dve(name):
                    act.wait_ge(gru_dve, 1 + at(t, GRU_DVE, name))
                wait_dve("pre_r")
                act.activation(rg[:, :, :], ar[:, :, :], ACT.Sigmoid).then_inc(gru_act, 1)
                wait_dve("pre_z")
                act.activation(zg[:, :, :], az[:, :, :], ACT.Sigmoid).then_inc(gru_act, 1)
                act.activation(zcg[:, :, :], az[:, :, :], ACT.Sigmoid, scale=-1.0).then_inc(gru_act, 1)
                wait_dve("pre_n")
                act.activation(ng[:, :, :], pn[:, :, :], ACT.Tanh).then_inc(gru_act, 1)
                if not last and s_ >= 2:
                    gates_out(j + 1, s_ - 2)

            act.activation(gb[:, 6:7], gb[:, 0:1], ACT.Sigmoid)
            with act.Fori(0, NG - 1) as j:
                for s_ in range(8):
                    recur(8 * j + s_, j, s_, False)
            for s_ in range(8):
                recur(8 * (NG - 1) + s_, NG - 1, s_, True)

            for k in range(KC):
                act.wait_ge(p_dve, at(0, POOL_DVE, f"keys{k}"))
                act.activation(keys2[:, k, :], keys[:, k, :], ACT.Square).then_inc(p_act, 1)
            act.wait_ge(p_pe, 2)
            act.activation(s_rs[:, :], ps[:, OB[0], :], ACT.Sqrt, bias=eps_t[:, 0:1]).then_inc(p_act, 1)
            act.wait_ge(p_dve, at(0, POOL_DVE, "score_sub"))
            act.activation(s_at[:, :, :], s_at[:, :, :], ACT.Exp).then_inc(p_act, 1)

            def squares(j):
                act.wait_ge(p_y, j + 1)
                act.activation(quarter(yt2, j), quarter(yt, j), ACT.Square).then_inc(p_sq, 1)

            def deviation(j):
                act.wait_ge(p_var, j + 1)
                act.activation(frs4[:, 8 * j:8 * j + 8, :].rearrange("p t b -> p (t b)"), ps[:, VAR_BANK[j], :], ACT.Sqrt,
                               bias=eps_t[:, 0:1]).then_inc(p_dev, 1)

            def affine(j):
                act.wait_ge(*((p_norm, j + 1) if j < 3 else (p_norm3, 1)))
                for c in range(KC):
                    r = act.activation(quarter(yt, j, c), quarter(yt, j, c), ACT.Identity, scale=col("ln_gamma", c),
                                       bias=col("ln_beta", c))
                r.then_inc(p_aff, 1)

            for j in range(3):
                squares(j)
            deviation(0)
            squares(3)
            deviation(1)
            deviation(2)
            affine(0)
            deviation(3)
            for j in range(1, 4):
                affine(j)

            act.activation(gb[:, 7:8], gb[:, 0:1], ACT.Tanh)
            act.wait_ge(rk0, 2)
            with act.Fori(0, T) as t:
                for k in range(4):
                    qk_ = rk[("q", "q2", "q3", "q4")[k]]
                    if k:
                        act.wait_ge(rk_dve, RK_START + at(t, RK_DVE, ("q2", "q3", "q4")[k - 1]))
                    else:
                        act.wait_ge(rk_dve, RK_START + len(RK_DVE) * t - 2)
                    act.activation(rk["th"][:, :, :], qk_[:, :, :], ACT.Tanh).then_inc(rk_act, 1)
                    act.activation(rk["qsq"][:, :, :], qk_[:, :, :], ACT.Square).then_inc(rk_act, 1)

        @block.vector
        def _(dve):
            start_counts(dve, "dve")
            dve.memset(idle[:, :], 0.0)
            dve.memset(ones[:, :], 1.0 / D)
            dve.memset(eps_t[:, :], LN_EPS).then_inc(consts, 1)

            def ln_center(g):
                dve.wait_ge(ln_pe, 2 * g + 1)
                if not isinstance(g, int) or g:
                    dve.wait_ge(x1_lo, g)
                dve.tensor_tensor(xc[:, :, :], group(x_all, g),
                                  ps[:, TB, :].unsqueeze(1).to_broadcast([P, KC, GT]), ALU.subtract).then_inc(ln_dve, 1)

            def ln_recip(g):
                dve.wait_ge(ln_act, 2 * g + 2)
                dve.reciprocal(rs[:, :], rs[:, :]).then_inc(ln_dve, 1)

            def low(g):
                dve.wait_ge(x1_hi, g + 1)
                dve.tensor_tensor(x_lo[:, :, :], xc[:, :, :], x_hi[:, :, :].bitcast(F32), ALU.subtract).then_inc(x1_lo, 1)

            def key(n, u, h):
                dve.wait_ge(proj_done, 12 * n + 2 * h + 2)
                if h >= 2 or not (isinstance(n, int) and n == 0):
                    dve.wait_ge(scores_done, 4 * n + h - 1)
                dve.tensor_scalar(qk[:, 1, h % 2, :], ps[:, PJ[1], :], col("qkv_b", HEADS + HU * u + h), None,
                                  ALU.add).then_inc(dve_evac, 1)

            def value(n, i):
                dve.wait_ge(proj_done, 12 * n + 8 + i + 1)
                if not (isinstance(n, int) and n == 0):
                    dve.wait_ge(pv_done, 1 + 4 * n)
                dve.tensor_copy(V[:, i, :], ps[:, PJ[1], :]).then_inc(dve_evac, 1)

            def out_low(U, u, h):
                dve.wait_ge(ohi_done, 4 * U + h + 1)
                dve.scalar_tensor_tensor(o_lo[:, h % 2, :], ps[:, OB[h % 2], :], col("qkv_b", 2 * HEADS + HU * u + h),
                                         o_hi[:, h % 2, :].bitcast(F32), ALU.add, ALU.subtract).then_inc(olo_done, 1)

            def soft_wait(U, name):
                dve.wait_ge(soft, at(U, SOFT, name))

            S = ps[:, SB, :].rearrange("p (a s) -> p a s", s=T)
            whole = [P, NT * HU, T]

            def soft_a(U):
                dve.wait_ge(scores_done, 4 * U + 4)
                dve.reduce_max(mx[:, :], S, axis=AX.X).then_inc(soft, 1)
                soft_wait(U, "max")
                dve.tensor_tensor(Pr[:, :, :], S, mx[:, :].unsqueeze(2).to_broadcast(whole), ALU.subtract).then_inc(soft, 1)

            def soft_b(U):
                dve.wait_ge(exp_done, U + 1)
                dve.reduce_sum(sm[:, :], Pr[:, :, :], axis=AX.X).then_inc(soft, 1)
                soft_wait(U, "sum")
                dve.reciprocal(sm[:, :], sm[:, :]).then_inc(soft, 1)
                soft_wait(U, "recip")
                dve.tensor_tensor(Pr[:, :, :], Pr[:, :, :], sm[:, :].unsqueeze(2).to_broadcast(whole), ALU.mult).then_inc(soft, 1)

            def soft_c(U):
                soft_wait(U, "norm")
                dve.wait_ge(pv_done, 1 + 4 * U)
                for j in range(BT):
                    js = slice(j * T, j * T + T)
                    dve.transpose(BD[js, :, js], Pr[js, :, :]).then_inc(soft, 1)

            def l2_center(g):
                dve.wait_ge(l2_pe, 2 * g + 1)
                if not isinstance(g, int) or g:
                    dve.wait_ge(m_lo_s, g)
                dve.tensor_tensor((xc if isinstance(g, int) and g == 0 else fc)[:, :, :], group(x_all, g),
                                  ps[:, TB, :].unsqueeze(1).to_broadcast([P, KC, GT]), ALU.subtract).then_inc(l2_dve, 1)

            def l2_recip(g):
                dve.wait_ge(l2_act, 2 * g + 2)
                f = rs if isinstance(g, int) and g == 0 else frs
                dve.reciprocal(f[:, :], f[:, :]).then_inc(l2_dve, 1)

            def m_low(g):
                dve.wait_ge(m_hi_s, g + 1)
                dve.tensor_tensor(m_lo[:, :, :], (xc if isinstance(g, int) and g == 0 else fc)[:, :, :], m_hi[:, :, :].bitcast(F32), ALU.subtract).then_inc(m_lo_s, 1)

            def gate(g):
                scratch = Pr[:, :, :].rearrange("p a s -> p (a s)")
                dve.wait_ge(out_done, 1 + 16 * g + 16)
                for c in range(KC):
                    if c:
                        dve.wait_ge(gate_done, 1 + at(g, GATE, "add0"))
                    dve.scalar_tensor_tensor(by_batch(scratch), by_batch(ps[:, YB[c], :]), col("out_b", c),
                                             ada_rows(GATE1, g, c), ALU.add, ALU.mult).then_inc(gate_done, 1)
                    dve.wait_ge(gate_done, 1 + at(g, GATE, f"gate{c}"))
                    dve.tensor_tensor(group(x_all, g, c), group(x_all, g, c), scratch, ALU.add).then_inc(gate_done, 1)

            ln_center(0)
            dve.wait_ge(ld_v, 32)
            dve.wait_ge(ada_mm, 1)
            for j in range(12):
                one = 1.0 if j // 2 in (SCALE1, SCALE2) else 0.0
                r = dve.tensor_scalar(ada[:, j, :], ps[:, YB[j // 6], (j % 6) * B:(j % 6) * B + B], col("ada_b", j), one,
                                      ALU.add, ALU.add)
            r.then_inc(ada_dn, 1)
            ln_recip(0)
            for kc, src in enumerate((BD[:, 0:12, :].rearrange("p a b -> p (a b)"),
                                      stage[:, :, :].rearrange("p a b -> p (a b)"))):
                dve.wait_ge(w_hi0, kc + 1)
                dve.tensor_tensor(W_lo[:, 0, kc, :, :].rearrange("p a b -> p (a b)"), src,
                                  W_hi[:, 0, kc, :, :].rearrange("p a b -> p (a b)").bitcast(F32),
                                  ALU.subtract).then_inc(w_rdy, 1)
            dve.wait_ge(w_rdy, 1)
            dve.memset(BD[:, :, :], 0.0).then_inc(ada_dn, 1)
            low(0)
            for h in range(HU):
                key(0, 0, h)
            value(0, 1)
            value(0, 3)
            dve.wait_ge(ada_dn, 2)

            def attention(g, last):
                for u in range(NU):
                    U = NU * g + u
                    n, un = U + 1, (u + 1) % NU
                    project = not (last and u == NU - 1)
                    if u == NU - 1 and not last:
                        low(g + 1)
                    soft_a(U)
                    if project:
                        key(n, un, 0)
                    soft_b(U)
                    if project:
                        key(n, un, 1)
                    if u == 0 and not last:
                        ln_center(g + 1)
                    if u == 1 and not last:
                        ln_recip(g + 1)
                    if u == 1 and last:
                        l2_center(0)
                    if u == 2 and last:
                        l2_recip(0)
                    soft_c(U)
                    if project:
                        key(n, un, 2)
                    out_low(U, u, 0)
                    out_low(U, u, 1)
                    if project:
                        key(n, un, 3)
                    out_low(U, u, 2)
                    out_low(U, u, 3)
                    if project:
                        value(n, 1)
                        value(n, 3)
                    if u == NU - 1 and last:
                        m_low(0)
                        dve.wait_ge(fw_hi, 1)
                        dve.tensor_tensor(f1_lo[:, :, :], f1_raw[:, :, :], f1_hi[:, :, :].bitcast(F32),
                                          ALU.subtract).then_inc(fw_lo, 1)
                    if u == NU - 1:
                        gate(g)

            with dve.Fori(0, NG - 1) as g:
                attention(g, False)
            attention(NG - 1, True)

            def ffn(g, last):
                for m in range(MC):
                    dve.wait_ge(gel_done, 1 + 2 * (MC * g + m) + 2)
                    dve.tensor_tensor(g_lo[:, m, :], gel[:, m % 2, :], g_hi[:, m, :].bitcast(F32),
                                      ALU.subtract).then_inc(glo_done, 1)
                    if m == 1 and not last:
                        l2_center(g + 1)
                    if m == 5 and not last:
                        l2_recip(g + 1)
                if not last:
                    m_low(g + 1)
                for c in range(KC):
                    dve.wait_ge(down_done, 1 + KC * g + c + 1)
                    dve.wait_ge(ffn_out, 1 + 4 * g + 2 * c)
                    dve.scalar_tensor_tensor(by_batch(ysc[:, :]), by_batch(ps[:, YB[c], :]), col("ffn_b2", c),
                                             ada_rows(GATE2, g, c), ALU.add, ALU.mult).then_inc(fgate, 1)

            dve.wait_ge(fw_hi, 2)
            dve.tensor_tensor(f2_lo[:, :, :], f2_raw[:, :, :], f2_hi[:, :, :].bitcast(F32), ALU.subtract).then_inc(fw_lo, 1)
            with dve.Fori(0, NG - 1) as g:
                ffn(g, False)
            ffn(NG - 1, True)

            dve.wait_ge(iw_hi, 1)
            dve.tensor_tensor(ih_lo[:, :, :], ih_raw[:, :, :], ih_hi[:, :, :].bitcast(F32), ALU.subtract).then_inc(iw_lo, 1)
            dve.wait_ge(down_done, 1 + KC * NG)
            dve.wait_ge(glo_done, 1 + MC * NG)
            for c in range(KC):
                dve.wait_ge(y0_hi, c + 1)
                r = dve.tensor_tensor(y_lo[:, c, 0:GT], quarter(xtb, 0, c), y_hi[:, c, 0:GT].bitcast(F32), ALU.subtract)
                r.then_inc(y_split, 1)
            dve.tensor_copy(gb[:, 4:6], vec[:, VEC["b_ih"] + 4:VEC["b_ih"] + 6])
            dve.tensor_tensor(gb[:, 0:4], vec[:, VEC["b_ih"]:VEC["b_ih"] + 4], vec[:, VEC["b_hh"]:VEC["b_hh"] + 4], ALU.add)
            dve.tensor_copy(bhn[:, :, :], vec[:, VEC["b_hh"] + 4:VEC["b_hh"] + 6].unsqueeze(2).to_broadcast([P, KC, B]))
            dve.tensor_copy(ht[:, :, :], cnd[:, :, :]).then_inc(h0, 1)
            dve.wait_ge(h0, 1)
            def recur(t):
                def half(bank):
                    return ps[:, bank, 0:KC * B].rearrange("p (c b) -> p c b", b=B)

                def gates(part):
                    return gi[:, KC * part:KC * part + KC, bass.ds(t, 1), :].rearrange("p c t b -> p c (t b)")

                def mine(name):
                    dve.wait_ge(gru_dve, 1 + at(t, GRU_DVE, name))

                dve.wait_ge(gru_pe, at(t, GRU_PE, "r"))
                dve.tensor_tensor(ar[:, :, :], half(SB), gates(0), ALU.add).then_inc(gru_dve, 1)
                dve.wait_ge(gru_act, at(t, GRU_ACT, "r"))
                dve.tensor_tensor(rb[:, :, :], rg[:, :, :], bhn[:, :, :], ALU.mult).then_inc(gru_dve, 1)
                mine("r_bias")
                dve.tensor_tensor(nb[:, :, :], rb[:, :, :], gates(2), ALU.add).then_inc(gru_dve, 1)
                dve.wait_ge(gru_pe, at(t, GRU_PE, "z"))
                dve.tensor_tensor(az[:, :, :], half(OB[0]), gates(1), ALU.add).then_inc(gru_dve, 1)
                dve.wait_ge(gru_pe, at(t, GRU_PE, "hn"))
                dve.tensor_tensor(rn[:, :, :], half(OB[1]), rg[:, :, :], ALU.mult).then_inc(gru_dve, 1)
                mine("r_hn")
                dve.tensor_tensor(pn[:, :, :], rn[:, :, :], nb[:, :, :], ALU.add).then_inc(gru_dve, 1)
                dve.wait_ge(gru_act, at(t, GRU_ACT, "z"))
                dve.tensor_tensor(zh[:, :, :], zg[:, :, :], ht[:, :, :], ALU.mult).then_inc(gru_dve, 1)
                dve.wait_ge(gru_act, at(t, GRU_ACT, "n"))
                dve.tensor_tensor(zn[:, :, :], ng[:, :, :], zcg[:, :, :], ALU.mult).then_inc(gru_dve, 1)
                dve.wait_ge(gru_out, 1 + t)
                mine("zc_n")
                dve.tensor_tensor(ht[:, :, :], zn[:, :, :], zh[:, :, :], ALU.add).then_inc(gru_dve, 1)

            with dve.Fori(0, T // 8) as j:
                dve.wait_ge(gi_act, 1 + 6 * (j + 1))
                for s_ in range(8):
                    recur(8 * j + s_)

            dve.wait_ge(gru_out, 1 + T)
            dve.wait_ge(blk_done, 3 * NBLK)
            dve.wait_ge(gru_dve, 1 + len(GRU_DVE) * T)

            def step(name, r):
                r.then_inc(p_dve, 1)

            def done(name):
                dve.wait_ge(p_dve, at(0, POOL_DVE, name))

            def center(j):
                dve.wait_ge(p_mean, j + 1)
                dve.tensor_tensor(quarter(yt, j), quarter(xtb, j),
                                  ps[:, MEAN_BANK[j], :].unsqueeze(1).to_broadcast([P, KC, GT]), ALU.subtract).then_inc(p_cen, 1)

            spread = [P, NBLK, B]
            step("score_vec", dve.tensor_tensor(s_mx[:, 0, 0:KC], vec[:, VEC["rms_w"]:VEC["rms_w"] + KC], cnd[:, :, 1], ALU.mult))
            step("wo_sum", dve.reduce_sum(wo_m[:, :], wo_sb[:, :, :], axis=AX.X))
            done("score_vec")
            step("wqr", dve.tensor_copy(wqr[:, :, :], s_mx[:, 0, 0:KC].unsqueeze(2).to_broadcast([P, KC, P])))
            for c in range(KC):
                dve.wait_ge(p_keys, 2)
                step(f"keys{c}", dve.tensor_copy(keys[:, c, :], ps[:, PJ[c], :]))
            done("wo_sum")
            step("wo_mean", dve.tensor_scalar(wo_m[:, :], wo_m[:, :], 1.0 / D, None, ALU.mult))
            done("wo_mean")
            step("wo_c", dve.tensor_tensor(wo_c[:, :, :], wo_sb[:, :, :], wo_m[:, :].unsqueeze(2).to_broadcast([P, KC, D]),
                                           ALU.subtract))
            center(0)
            center(1)
            dve.wait_ge(p_act, 3)
            step("rms_inv", dve.reciprocal(s_rs[:, :], s_rs[:, :]))
            done("rms_inv")
            dve.wait_ge(p_pe, 1)
            step("score", dve.tensor_tensor(s_sc[:, :, :].rearrange("p n b -> p (n b)"), ps[:, SB, :], s_rs[:, :], ALU.mult))
            done("score")
            step("score_max", dve.reduce_max(s_mx[:, 1, :], s_sc[:, :, :].rearrange("p n b -> p b n"), axis=AX.X))
            done("score_max")
            step("score_sub", dve.tensor_tensor(s_at[:, :, :], s_sc[:, :, :], s_mx[:, 1, :].unsqueeze(1).to_broadcast(spread),
                                                ALU.subtract))
            center(2)
            dve.wait_ge(p_act, 4)
            step("sum", dve.reduce_sum(s_mx[:, 0, :], s_at[:, :, :].rearrange("p n b -> p b n"), axis=AX.X))
            done("sum")
            step("recip", dve.reciprocal(s_mx[:, 0, :], s_mx[:, 0, :]))
            for c in range(KC):
                if c:
                    done("att_sum0")
                step(f"att_mul{c}", dve.tensor_tensor(s_wb[:, :, :], blk[:, c, :, :], s_at[:, :, :], ALU.mult))
                done(f"att_mul{c}")
                step(f"att_sum{c}", dve.reduce_sum(att[:, c, :], s_wb[:, :, :].rearrange("p n b -> p b n"), axis=AX.X))
                done(f"att_sum{c}")
                step(f"att{c}", dve.tensor_tensor(att[:, c, :], att[:, c, :], s_mx[:, 0, :], ALU.mult))
            center(3)
            dve.wait_ge(p_pe, 3)
            for j in range(4):
                dve.wait_ge(p_cen, j + 1)
                q4 = yt[:, :, 8 * j:8 * j + 8, :]
                for c in range(KC):
                    r = dve.tensor_tensor(q4[:, c], q4[:, c],
                                          ps[:, OB[1], c * B:c * B + B].unsqueeze(1).to_broadcast([P, 8, B]), ALU.add)
                r.then_inc(p_y, 1)

            def inverse(j):
                f4 = frs4[:, 8 * j:8 * j + 8, :]
                dve.wait_ge(p_dev, j + 1)
                dve.reciprocal(f4, f4).then_inc(p_inv, 1)

            for j in range(4):
                inverse(j)
            dve.wait_ge(p_inv, 4)
            dve.tensor_tensor(quarter(yt, 3), quarter(yt, 3), by_row(frs4, 3), ALU.mult).then_inc(p_norm3, 1)

            dve.tensor_copy(rk["q"][:, :, :], cnd[:, :, :])
            dve.wait_ge(rk_pool, 2)
            dve.tensor_tensor(rk["e_a"][:, :, :], rk["d_row"][:, :, :], cnd[:, :, :], ALU.subtract).then_inc(rk0, 1)
            dve.wait_ge(p_aff, 4)
            dve.tensor_tensor(quarter(xtb, 3), quarter(xtb, 3), quarter(yt, 3), ALU.add).then_inc(rk0, 1)
            dve.wait_ge(rk0, 2)
            r_ = {n: rk[n][:, :, :] for n in rk}
            STT = dve.scalar_tensor_tensor
            with dve.Fori(0, T) as t:
                def mine(name):
                    dve.wait_ge(rk_dve, RK_START + at(t, RK_DVE, name))

                def pool(name):
                    dve.wait_ge(rk_pool, 2 + at(t, RK_POOL, name))

                def sq_done(k):
                    dve.wait_ge(rk_act, 8 * t + 2 * k + 2)

                def a_of(k):
                    return ps[:, SB if k % 2 == 0 else OB[0], 0:KC * B].rearrange("p (c b) -> p c b", b=B)

                def inc(r):
                    r.then_inc(rk_dve, 1)

                M, Ad = ALU.mult, ALU.add
                names = ("q", "q2", "q3", "q4")
                es = ("e_a", "e_b", "e_c", "e_d")
                coef = (DT / 2, DT / 2, DT)
                for k in range(3):
                    ck, pk = coef[k], coef[k] * EPSILON
                    if k:
                        mine(f"e{k + 1}")
                    else:
                        dve.wait_ge(rk_dve, RK_START + len(RK_DVE) * t)
                    inc(STT(r_["Z"], r_[es[k]], ck, r_["q"], M, Ad))
                    sq_done(k)
                    inc(STT(r_["w"], r_["qsq"], -3.0, r_[names[k]], Ad, M))
                    if k == 2:
                        pool("R1t")
                        inc(STT(r_["R"], r_["q3"], 2 / 3, r_["R1t"], M, Ad))
                    mine(f"w{k + 1}")
                    inc(STT(r_["Bk"], r_["w"], -ck / 3, r_["Z"], M, Ad))
                    pool("Ea" if k < 2 else "Eb")
                    inc(STT(r_["M"], r_[es[k]], -pk * BETA, r_["Ea" if k < 2 else "Eb"], M, Ad))
                    mine(f"M{k + 1}")
                    inc(STT(r_[es[k + 1]], r_[names[k]], -pk, r_["M"], M, Ad))
                    dve.wait_ge(rk_pe, 4 * t + k + 1)
                    mine(f"B{k + 1}")
                    inc(STT(r_[names[k + 1]], a_of(k), ck, r_["Bk"], M, Ad))
                c4 = DT / 6
                mine("e4")
                inc(STT(r_["Z"], r_["e_d"], c4, r_["R"], M, Ad))
                pool("S2")
                inc(STT(r_["S3"], r_["e_d"], -(1 - A_P * BETA), r_["S2"], M, Ad))
                sq_done(3)
                inc(STT(r_["w"], r_["qsq"], -3.0 - 1 / c4, r_["q4"], Ad, M))
                mine("w4")
                inc(STT(r_["Bk"], r_["w"], -c4 / 3, r_["Z"], M, Ad))
                mine("S3")
                inc(STT(r_["S4"], r_["q4"], A_P, r_["S3"], M, Ad))
                mine("S4")
                inc(STT(r_["pr"], r_["S4"], 1 / 3, r_["h_row"], M, Ad))
                dve.wait_ge(rk_pe, 4 * t + 4)
                mine("B4")
                inc(STT(r_["qraw"], a_of(3), c4, r_["Bk"], M, Ad))
                mine("q_raw")
                inc(dve.tensor_scalar(r_["q"], r_["qraw"], CLAMP, -CLAMP, ALU.min, ALU.max))
                mine("p_raw")
                inc(dve.tensor_scalar(r_["p"], r_["pr"], CLAMP, -CLAMP, ALU.min, ALU.max))
                mine("p")
                inc(dve.tensor_tensor(r_["e_a"], r_["d_row"], r_["p"], ALU.subtract))

        @block.gpsimd
        def _(pool):
            start_counts(pool, "pool")
            TT, TS = pool.tensor_tensor, pool.tensor_scalar

            def modulate(buf, factors, which_scale, which_shift, g, s_dve, s_pool):
                pool.wait_ge(s_dve, 2 * g + 2)
                TT(buf[:, :, :], buf[:, :, :], factors[:, :].unsqueeze(1).to_broadcast([P, KC, GT]), ALU.mult).then_inc(s_pool, 1)
                pool.wait_ge(s_pool, 3 * g + 1)
                b4 = buf[:, :, :].rearrange("p c (b t) -> p c b t", t=T)
                for i, (which, op) in enumerate(((which_scale, ALU.mult), (which_shift, ALU.add))):
                    for c in range(KC):
                        r = TT(b4[:, c], b4[:, c], ada_rows(which, g, c), op)
                    r.then_inc(s_pool, 1)
                    if i == 0:
                        pool.wait_ge(s_pool, 3 * g + 2)

            pool.wait_ge(ada_dn, 1)
            modulate(xc, rs, SCALE1, SHIFT1, 0, ln_dve, ln_pool)
            n = 0

            def split(hi, lo, src):
                nonlocal n
                pool.wait_ge(ld_stage, 16 * (n + 1))
                TS(hi, src, 1.0, 0.0, ALU.mult, ALU.add).then_inc(pool_w, 1)
                pool.wait_ge(pool_w, 2 * n + 1)
                TT(lo, src, hi.bitcast(F32), ALU.subtract).then_inc(pool_w, 1)
                n += 1

            flat = stage[:, :, :].rearrange("p a b -> p (a b)")
            for u in range(1, NU + 1):
                for kc in range(KC if u < NU else 0):
                    split(W_hi[:, u, kc, :, :].rearrange("p a b -> p (a b)"),
                          W_lo[:, u, kc, :, :].rearrange("p a b -> p (a b)"), flat)
                hs = slice(HU * (u - 1), HU * u)
                split(wo_hi[:, hs, :].rearrange("p a b -> p (a b)"), wo_lo[:, hs, :].rearrange("p a b -> p (a b)"),
                      flat[:, 0:HU * D])

            with pool.Fori(1, NG) as g:
                modulate(xc, rs, SCALE1, SHIFT1, g, ln_dve, ln_pool)

            def finish(g):
                for c in range(KC):
                    pool.wait_ge(fgate, 1 + KC * g + c + 1)
                    TT(ysc[:, :], ysc[:, :], group(x_all, g, c), ALU.add).then_inc(ffn_out, 1)
                    if c == 0:
                        pool.wait_ge(ld_late, 96)
                    pool.wait_ge(ffn_out, 1 + 4 * g + 2 * c + 1)
                    dst = xtb[:, c, 0:T, bass.ds(g * GB, GB)] if not isinstance(g, int) else xtb[:, c, 0:T, g * GB:g * GB + GB]
                    TT(dst.rearrange("p t b -> p b t"), by_batch(ysc[:, :]), by_batch(group(xorig, g, c)),
                       ALU.add).then_inc(ffn_out, 1)

            modulate(xc, rs, SCALE2, SHIFT2, 0, l2_dve, l2_pool)
            with pool.Fori(0, NG - 1) as g:
                modulate(fc, frs, SCALE2, SHIFT2, g + 1, l2_dve, l2_pool)
                finish(g)
            finish(NG - 1)

            def split_inputs(j):
                t8, at8 = (slice(0, 8), slice(0, GT)) if isinstance(j, int) else (bass.ds(8 * j, 8), bass.ds(GT * j, GT))
                for c in range(KC):
                    r = pool.tensor_copy(y_hi[:, c, at8], xtb[:, c, t8, :].rearrange("p t b -> p (t b)"))
                r.then_inc(y_split, 1)
                pool.wait_ge(y_split, 2 * j + 1)
                TT(y_lo[:, :, at8], xtb[:, :, t8, :].rearrange("p c t b -> p c (t b)"), y_hi[:, :, at8].bitcast(F32),
                   ALU.subtract).then_inc(y_split, 1)

            def keep_state(j, s_):
                t = 8 * j + s_

                def row_(i):
                    return xtb[:, :, i, :] if isinstance(i, int) else xtb[:, :, bass.ds(i, 1), :].rearrange("p c t b -> p c (t b)")

                pool.wait_ge(gru_dve, 1 + len(GRU_DVE) * t + len(GRU_DVE))
                TT(row_(t), row_(t), ht[:, :, :], ALU.add).then_inc(gru_out, 1)
                i, n = s_ % BLK, (8 // BLK) * j + s_ // BLK
                if i:
                    pool.wait_ge(gru_out, 1 + t + 1)
                    if i > 1:
                        pool.wait_ge(blk_done, (BLK - 1) * n + i - 1)
                    pool.sem_inc(blk_turn, 1)
                if i == 1:
                    TT(blk_part[:, :, :], row_(t), row_(t - 1), ALU.add).then_inc(blk_done, 1)
                elif i:
                    to = blk_part[:, :, :] if i < BLK - 1 else blk[:, :, n, :] if isinstance(n, int) else \
                        blk[:, :, bass.ds(n, 1), :].rearrange("p c n b -> p c (n b)")
                    TT(to, blk_part[:, :, :], row_(t), ALU.add).then_inc(blk_done, 1)

            pool.wait_ge(ffn_out, 1 + 4 * NG)
            pool.wait_ge(down_done, 1 + KC * NG)
            with pool.Fori(0, NG - 1) as j:
                for s_ in range(8):
                    keep_state(j, s_)
                    if s_ == 0:
                        split_inputs(j + 1)
            for s_ in range(8):
                keep_state(NG - 1, s_)

            pool.memset(xtb[:, :, T, :], 0.0)
            def normalise(j):
                pool.wait_ge(p_inv, j + 1)
                TT(quarter(yt, j), quarter(yt, j), by_row(frs4, j), ALU.mult).then_inc(p_norm, 1)

            def add_in(j):
                pool.wait_ge(p_aff, j + 1)
                TT(quarter(xtb, j), quarter(xtb, j), quarter(yt, j), ALU.add).then_inc(p_add, 1)

            normalise(0)
            normalise(1)
            add_in(0)
            normalise(2)
            pool.memset(rk["third"][:, :, :], 1 / 3)
            r_ = {n: rk[n][:, :, :] for n in rk}
            l3_bias = vec[:, VEC["l3_bias"]:VEC["l3_bias"] + KC].unsqueeze(2).to_broadcast([P, KC, B])
            pool.wait_ge(p_add, 1)
            TT(r_["d_row"], xtb[:, :, 0, :], l3_bias, ALU.add).then_inc(rk_pool, 1)
            pool.wait_ge(rk_pool, 1)
            TS(r_["g_row"], r_["d_row"], A_P * BETA, -A_P * ALPHA, ALU.mult, ALU.add).then_inc(rk_pool, 1)
            add_in(1)
            add_in(2)

            pool.wait_ge(rk0, 2)
            pool.wait_ge(p_add, 3)
            with pool.Fori(0, T) as t:
                def at_step(tile, i):
                    return tile[:, :, bass.ds(i, 1), :].rearrange("p c t b -> p c (t b)")

                def dve_(name):
                    pool.wait_ge(rk_dve, RK_START + at(t, RK_DVE, name))

                def mine(name):
                    pool.wait_ge(rk_pool, 2 + at(t, RK_POOL, name))

                pool.wait_ge(rk_dve, RK_START + len(RK_DVE) * t)
                pool.wait_ge(rk_pool, 2 + len(RK_POOL) * t)
                TT(r_["Ea"], r_["e_a"], r_["g_row"], ALU.add).then_inc(rk_pool, 1)
                mine("Ea")
                TT(r_["Eb"], r_["Ea"], r_["g_row"], ALU.add).then_inc(rk_pool, 1)
                TS(r_["h_row"], r_["d_row"], 1 - A_P * BETA / 3, A_P * ALPHA / 3, ALU.mult, ALU.add).then_inc(rk_pool, 1)
                dve_("q2")
                TT(r_["R1"], r_["q2"], r_["q"], ALU.subtract).then_inc(rk_pool, 1)
                mine("R1")
                TT(r_["R1t"], r_["R1"], r_["third"], ALU.mult).then_inc(rk_pool, 1)
                TT(r_["d_row"], at_step(xtb, t + 1), l3_bias, ALU.add).then_inc(rk_pool, 1)
                TT(r_["S1"], r_["e_a"], r_["e_b"], ALU.subtract).then_inc(rk_pool, 1)
                dve_("e3")
                mine("S1")
                TT(r_["S1b"], r_["S1"], r_["e_c"], ALU.subtract).then_inc(rk_pool, 1)
                TS(r_["g_row"], r_["d_row"], A_P * BETA, -A_P * ALPHA, ALU.mult, ALU.add).then_inc(rk_pool, 1)
                mine("S1b")
                TT(r_["S2"], r_["S1b"], r_["e_c"], ALU.subtract).then_inc(rk_pool, 1)
                xt = xtb[:, :, bass.ds(t, 1), :].rearrange("p c t b -> p c (t b)")
                dve_("q")
                TT(xt, xt, r_["q"], ALU.add).then_inc(rk_out, 1)


def _features(a):
    a = np.asarray(a)
    return np.moveaxis(a.reshape(-1, P, *a.shape[1:]), 0, 1)


def kernel(**inputs):
    import concourse.bacc as bacc
    from concourse.bass_utils import run_bass_kernel_spmd

    a = {k: np.asarray(v) for k, v in inputs.items()}
    qkv = a["L0_cond_qkv_w"].reshape(KC, P, 3, NU, HU * DH)
    arrays = {
        "xT": _features(a["x"].reshape(TOK, D).T),
        "cond": _features(a["cond_2048"].T),
        "ada_w": _features(a["L0_cond_ada_w"]),
        "qkv_w": qkv.transpose(3, 1, 0, 2, 4).reshape(NU, P, KC, 3 * HU * DH),
        "out_w": _features(a["L0_cond_out_w"]).reshape(P, HEADS * D),
        "ffn_w1": _features(a["L0_cond_ffn_w1"]),
        "ffn_w2": _features(a["L0_cond_ffn_w2"]),
        "w_ih": _features(a["L1_cond_W_ih"]),
        "w_hh": _features(a["L1_cond_W_hh"]),
        "wk": _features(a["L2_cond_Wk"].T),
        "wo": _features(a["L2_cond_Wo"].T),
        "coup": _features(a["L3_cond_coupling"].T),
        "vecs": np.concatenate([_features(a[n]) for n in (
            "L0_cond_ada_b", "L0_cond_qkv_b", "L0_cond_out_b", "L0_cond_ffn_b1", "L0_cond_ffn_b2", "L1_cond_b_ih",
            "L1_cond_b_hh", "L2_cond_rms_weight", "L2_cond_ln_gamma", "L2_cond_ln_beta", "L3_cond_bias")], axis=1),
    }
    arrays = {k: np.ascontiguousarray(v) for k, v in arrays.items()}
    nc = bacc.Bacc("TRN2", target_bir_lowering=False, num_devices=1)
    args = [nc.dram_tensor(k, v.shape, mybir.dt.from_np(v.dtype), kind="ExternalInput").ap() for k, v in arrays.items()]
    out = nc.dram_tensor("out", (P, KC, T, B), F32, kind="ExternalOutput").ap()
    build(nc, *args, out)
    r = run_bass_kernel_spmd(nc, [arrays], core_ids=[0])
    o = np.asarray(r.results[0]["out"])
    return np.ascontiguousarray(o.transpose(3, 2, 1, 0)).reshape(B, T, D)
```
